# Optimizing a Trainium2 kernel written in Bass

```python
import numpy as np
import jax
import jax.numpy as jnp

def _softmax(x, axis=-1):
    return jax.nn.softmax(x, axis=axis)

def _gelu(x):
    return jax.nn.gelu(x, approximate=True)

def _silu(x):
    return jax.nn.silu(x)

def _sigmoid(x):
    return jax.nn.sigmoid(x)

def _layernorm(x, axis=-1, eps=1e-05):
    m = jnp.mean(x, axis=axis, keepdims=True)
    v = jnp.var(x, axis=axis, keepdims=True)
    return (x - m) / jnp.sqrt(v + eps)

def _scatter_add(tgt, idx, src, axis=0):
    return tgt.at[idx].add(src)

def _segment_sum(src, seg, n):
    return jax.ops.segment_sum(src, seg, n)
kernel_name = 'mk_macaron_d1_jaxref_r8_2a159a'

def setup_inputs(seed: int=0):
    np.random.seed(seed)
    _w = jnp.asarray

    def _L0_attn_setup():
        import jax, jax.numpy as jnp
        import numpy as np
        B, TT, C, H, T = (4, 512, 128, 16, 128)
        K = C // H
        HEAD_DIV = 8.0
        EPS = 1e-05
        LAYER_ID, N_LAYER = (12, 24)
        key = jax.random.key(seed)
        ks = jax.random.split(key, 8)
        r01 = LAYER_ID / (N_LAYER - 1)
        r1a0 = 1.0 - LAYER_ID / N_LAYER
        ddd = (jnp.arange(C, dtype=jnp.float32) / C).reshape(1, 1, C)
        h = jnp.arange(H, dtype=jnp.float32)
        scale = 0.02
        return {'xq': jax.random.normal(ks[0], (B, TT, C), jnp.float32), 'time_mix_k': ddd ** r1a0, 'time_mix_v': ddd ** r1a0 + 0.3 * r01, 'time_mix_r': ddd ** (0.5 * r1a0), 'time_mix_g': ddd ** (0.5 * r1a0), 'time_decay': -8.0 + 7.0 * (h / (H - 1)) ** (0.7 + 1.3 * r01), 'time_faaaa': r01 * (1.0 - h / (H - 1)), 'W_r': jax.random.normal(ks[1], (C, C), jnp.float32) * scale, 'W_k': jax.random.normal(ks[2], (C, C), jnp.float32) * scale, 'W_v': jax.random.normal(ks[3], (C, C), jnp.float32) * scale, 'W_g': jax.random.normal(ks[4], (C, C), jnp.float32) * scale, 'W_o': jax.random.normal(ks[5], (C, C), jnp.float32) * scale, 'ln_w': jnp.ones((C,), jnp.float32), 'ln_b': jnp.zeros((C,), jnp.float32)}
    _L0_attn_in = _L0_attn_setup()

    def _L0_ffn_setup():
        import jax, jax.numpy as jnp
        import numpy as np
        HIDDEN = 128
        INTER = 512
        NUM_EXPERTS = 8
        TOP_K = 2
        EPS = 1e-05

        def _layer_norm(x, g, b):
            m = jnp.mean(x, axis=-1, keepdims=True)
            v = jnp.mean(jnp.square(x - m), axis=-1, keepdims=True)
            return (x - m) * jax.lax.rsqrt(v + EPS) * g + b
        key = jax.random.key(seed)
        ks = jax.random.split(key, 8)
        s = 0.02
        return {'x': jax.random.normal(ks[0], (4, 256, HIDDEN), dtype=jnp.float32), 'ln1_g': jnp.ones((HIDDEN,), jnp.float32), 'ln1_b': jnp.zeros((HIDDEN,), jnp.float32), 'attn_w': jax.random.normal(ks[1], (HIDDEN, HIDDEN), jnp.float32) * s, 'ln2_g': jnp.ones((HIDDEN,), jnp.float32), 'ln2_b': jnp.zeros((HIDDEN,), jnp.float32), 'gate_w': jax.random.normal(ks[2], (NUM_EXPERTS, HIDDEN), jnp.float32) * s, 'gate_proj': jax.random.normal(ks[3], (NUM_EXPERTS, INTER, HIDDEN), jnp.float32) * s, 'up_proj': jax.random.normal(ks[4], (NUM_EXPERTS, INTER, HIDDEN), jnp.float32) * s, 'down_proj': jax.random.normal(ks[5], (NUM_EXPERTS, HIDDEN, INTER), jnp.float32) * s}
    _L0_ffn_in = _L0_ffn_setup()
    _d = {'L0_attn_xq': _L0_attn_in['xq'], 'L0_attn_time_mix_k': _L0_attn_in['time_mix_k'], 'L0_attn_time_mix_v': _L0_attn_in['time_mix_v'], 'L0_attn_time_mix_r': _L0_attn_in['time_mix_r'], 'L0_attn_time_mix_g': _L0_attn_in['time_mix_g'], 'L0_attn_time_decay': _L0_attn_in['time_decay'], 'L0_attn_time_faaaa': _L0_attn_in['time_faaaa'], 'L0_attn_W_r': _L0_attn_in['W_r'], 'L0_attn_W_k': _L0_attn_in['W_k'], 'L0_attn_W_v': _L0_attn_in['W_v'], 'L0_attn_W_g': _L0_attn_in['W_g'], 'L0_attn_W_o': _L0_attn_in['W_o'], 'L0_attn_ln_w': _L0_attn_in['ln_w'], 'L0_attn_ln_b': _L0_attn_in['ln_b'], 'L0_ffn_ln1_g': _L0_ffn_in['ln1_g'], 'L0_ffn_ln1_b': _L0_ffn_in['ln1_b'], 'L0_ffn_attn_w': _L0_ffn_in['attn_w'], 'L0_ffn_ln2_g': _L0_ffn_in['ln2_g'], 'L0_ffn_ln2_b': _L0_ffn_in['ln2_b'], 'L0_ffn_gate_w': _L0_ffn_in['gate_w'], 'L0_ffn_gate_proj': _L0_ffn_in['gate_proj'], 'L0_ffn_up_proj': _L0_ffn_in['up_proj'], 'L0_ffn_down_proj': _L0_ffn_in['down_proj']}
    _x0 = _d['L0_attn_xq']
    _d['L0_attn_xq'] = jax.random.normal(jax.random.fold_in(jax.random.key(seed), 1), (2, 2048, 128), dtype=_x0.dtype)
    del _x0
    return _d

def reference(L0_attn_xq, L0_attn_time_mix_k, L0_attn_time_mix_v, L0_attn_time_mix_r, L0_attn_time_mix_g, L0_attn_time_decay, L0_attn_time_faaaa, L0_attn_W_r, L0_attn_W_k, L0_attn_W_v, L0_attn_W_g, L0_attn_W_o, L0_attn_ln_w, L0_attn_ln_b, L0_ffn_ln1_g, L0_ffn_ln1_b, L0_ffn_attn_w, L0_ffn_ln2_g, L0_ffn_ln2_b, L0_ffn_gate_w, L0_ffn_gate_proj, L0_ffn_up_proj, L0_ffn_down_proj):

    def _L0_attn_ref(xq, time_mix_k, time_mix_v, time_mix_r, time_mix_g, time_decay, time_faaaa, W_r, W_k, W_v, W_g, W_o, ln_w, ln_b):
        import jax, jax.numpy as jnp
        import numpy as np
        B, TT, C, H, T = (4, 512, 128, 16, 128)
        K = C // H
        HEAD_DIV = 8.0
        EPS = 1e-05
        LAYER_ID, N_LAYER = (12, 24)
        x = xq
        B_, TT_, C_ = x.shape
        N = TT_ // T
        xx = jnp.pad(x, ((0, 0), (1, 0), (0, 0)))[:, :-1]
        xr = x * time_mix_r + xx * (1 - time_mix_r)
        xk = x * time_mix_k + xx * (1 - time_mix_k)
        xv = x * time_mix_v + xx * (1 - time_mix_v)
        xg = x * time_mix_g + xx * (1 - time_mix_g)
        r = (xr @ W_r.T).reshape(B_, TT_, H, K).transpose(0, 2, 1, 3)
        k = (xk @ W_k.T).reshape(B_, TT_, H, K).transpose(0, 2, 1, 3)
        v = (xv @ W_v.T).reshape(B_, TT_, H, K).transpose(0, 2, 1, 3)
        g = jax.nn.silu(xg @ W_g.T)
        decay = jnp.exp(-jnp.exp(time_decay))
        u = time_faaaa
        ws = decay ** T
        i_idx = jnp.arange(T)
        wb = decay[:, None] ** i_idx
        wk = decay[:, None] ** (T - 1 - i_idx)
        diff = i_idx[:, None] - i_idx[None, :]
        pw = decay[:, None, None] ** jnp.maximum(diff - 1, 0)
        w_mat = jnp.where(diff > 0, pw, 0.0) + jnp.eye(T, dtype=x.dtype) * u[:, None, None]
        rc = r.reshape(B_, H, N, T, K).transpose(2, 0, 1, 3, 4)
        kc = k.reshape(B_, H, N, T, K).transpose(2, 0, 1, 3, 4)
        vc = v.reshape(B_, H, N, T, K).transpose(2, 0, 1, 3, 4)
        s0 = jnp.zeros((B_, H, K, K), x.dtype)

        def step(s, chunk):
            rr, kk, vv = chunk
            att = jnp.einsum('bhik,bhjk->bhij', rr, kk) * w_mat
            out = att @ vv + jnp.einsum('bhik,bhkv->bhiv', rr, s) * wb[None, :, :, None]
            s_new = ws[None, :, None, None] * s + jnp.einsum('bhjk,bhjv->bhkv', kk * wk[None, :, :, None], vv)
            return (s_new, out)
        _, xo = jax.lax.scan(step, s0, (rc, kc, vc))
        xo = xo.transpose(1, 0, 3, 2, 4).reshape(B_, TT_, H, K)
        y = xo / HEAD_DIV
        mu = y.mean(-1, keepdims=True)
        var = y.var(-1, keepdims=True)
        y = (y - mu) / jnp.sqrt(var + EPS)
        y = y * ln_w.reshape(H, K) + ln_b.reshape(H, K)
        y = y.reshape(B_, TT_, C_)
        return y * g @ W_o.T

    def _L0_ffn_ref(x, ln1_g, ln1_b, attn_w, ln2_g, ln2_b, gate_w, gate_proj, up_proj, down_proj):
        import jax, jax.numpy as jnp
        import numpy as np
        HIDDEN = 128
        INTER = 512
        NUM_EXPERTS = 8
        TOP_K = 2
        EPS = 1e-05

        def _layer_norm(x, g, b):
            m = jnp.mean(x, axis=-1, keepdims=True)
            v = jnp.mean(jnp.square(x - m), axis=-1, keepdims=True)
            return (x - m) * jax.lax.rsqrt(v + EPS) * g + b
        B, S, H = x.shape
        h = x + jnp.einsum('bsh,oh->bso', _layer_norm(x, ln1_g, ln1_b), attn_w)
        t = _layer_norm(h, ln2_g, ln2_b).reshape(-1, H)
        T = t.shape[0]
        logits = jnp.einsum('th,eh->te', t, gate_w)
        top_vals, top_idx = jax.lax.top_k(logits, TOP_K)
        rw = jax.nn.softmax(top_vals, axis=-1)
        comb = jnp.zeros((T, NUM_EXPERTS), dtype=t.dtype)
        comb = comb.at[jnp.arange(T)[:, None], top_idx].add(rw)
        out = jnp.zeros_like(t)
        for e in range(NUM_EXPERTS):
            g = jnp.einsum('th,ih->ti', t, gate_proj[e])
            u = jnp.einsum('th,ih->ti', t, up_proj[e])
            oe = jnp.einsum('ti,hi->th', jax.nn.silu(g) * u, down_proj[e])
            out = out + comb[:, e:e + 1] * oe
        return h + out.reshape(B, S, H)
    x = L0_attn_xq
    x = x + 0.5 * _L0_ffn_ref(_layernorm(x, axis=-1), L0_ffn_ln1_g, L0_ffn_ln1_b, L0_ffn_attn_w, L0_ffn_ln2_g, L0_ffn_ln2_b, L0_ffn_gate_w, L0_ffn_gate_proj, L0_ffn_up_proj, L0_ffn_down_proj)
    x = x + _L0_attn_ref(_layernorm(x, axis=-1), L0_attn_time_mix_k, L0_attn_time_mix_v, L0_attn_time_mix_r, L0_attn_time_mix_g, L0_attn_time_decay, L0_attn_time_faaaa, L0_attn_W_r, L0_attn_W_k, L0_attn_W_v, L0_attn_W_g, L0_attn_W_o, L0_attn_ln_w, L0_attn_ln_b)
    x = x + 0.5 * _L0_ffn_ref(_layernorm(x, axis=-1), L0_ffn_ln1_g, L0_ffn_ln1_b, L0_ffn_attn_w, L0_ffn_ln2_g, L0_ffn_ln2_b, L0_ffn_gate_w, L0_ffn_gate_proj, L0_ffn_up_proj, L0_ffn_down_proj)
    return x

_drawn_inputs = setup_inputs


def setup_inputs(seed=0):
    import zlib

    import numpy as np

    out = dict(_drawn_inputs(seed))
    spreads = {'L0_attn_ln_w': (1.0, 0.6),
     'L0_attn_ln_b': (0.0, 0.8),
     'L0_ffn_ln1_g': (1.0, 0.579),
     'L0_ffn_ln1_b': (0.0, 0.581),
     'L0_ffn_ln2_g': (1.0, 0.6),
     'L0_ffn_ln2_b': (0.0, 0.8)}
    factors = {'L0_attn_time_mix_k': 8.0,
     'L0_attn_time_mix_v': 8.0,
     'L0_attn_time_mix_r': 8.0,
     'L0_attn_time_mix_g': 8.0,
     'L0_attn_time_decay': 6.255,
     'L0_attn_time_faaaa': 8.0,
     'L0_attn_W_r': 3.83,
     'L0_attn_W_k': 3.768,
     'L0_attn_W_v': 3.811,
     'L0_attn_W_g': 3.765,
     'L0_attn_W_o': 3.788,
     'L0_ffn_gate_w': 8.0,
     'L0_ffn_gate_proj': 8.0,
     'L0_ffn_up_proj': 8.0,
     'L0_ffn_down_proj': 8.0}
    for name, (base, spread) in spreads.items():
        noise = np.random.default_rng([zlib.crc32(name.encode()), seed]).standard_normal(out[name].shape)
        drawn = base * np.exp(spread * noise) if base else spread * noise
        out[name] = jnp.asarray(drawn.astype(out[name].dtype))
    for name, factor in factors.items():
        out[name] = (out[name] * factor).astype(out[name].dtype)
    return out
```

```python
from contextlib import ExitStack

import concourse.bass as bass
from concourse import mybir

F32 = mybir.dt.float32
I32 = mybir.dt.int32
ALU = mybir.AluOpType
ACT = mybir.ActivationFunctionType
AX = mybir.AxisListType.X

P = 128
C = 128
HALVES = 2
SEQ = 2048
T = SEQ // P
GROUP = 4
G = T // GROUP
E = 8
INTER = 512
CH = INTER // P
TOP = 2
HEADS = 16
HD = C // HEADS
HQ = 32 // HD
EPS = 1e-5
XT = (SEQ * TOP + E * (P - 1)) // P
SLOTS = XT * P
FILL = 3
BIG = 3.0e38
DECAY_MAX = 1.0e30
AG = 2
AT = AG * P
NQ = T // AG

CONST = {}
_at = 0
for _name, _width in (("ident", P), ("before", P), ("ones", P), ("later", P), ("gap", P), ("iota", P),
                      ("block", P), ("heads4", HQ), ("left", 1), ("rank", E), ("limit", T), ("tile", XT + 1)):
    CONST[_name] = (_at, _at + _width)
    _at += _width
NCONST = _at
COLS = ("ln1_g", "ln1_b", "ln2_g", "ln2_b", "mix_r", "mix_k", "mix_v", "mix_g", "decay")
ROWS = ("ln_w", "ln_b", "decay")
WEIGHTS = ("proj", "r", "k", "v", "g", "o")

ORD = ("A1", "B1", "A2", "B2")


class Chain:

    def __init__(self, eng, sem, base=0):
        self.eng, self.sem, self.base, self.n = eng, sem, base, 0

    def step(self, ins):
        ins.then_inc(self.sem, 1)
        self.n += 1

    def wait(self):
        self.eng.wait_ge(self.sem, self.base + self.n)


def steps(eng, first, lo, hi, last, unroll, step):
    assert (hi - lo) % unroll == 0
    for n in range(first, lo):
        step(n, n % unroll)
    with eng.Fori(0, (hi - lo) // unroll) as i:
        for k in range(unroll):
            step(i * unroll + (lo + k), (lo + k) % unroll)
    for n in range(hi, last + 1):
        step(n, n % unroll)


def known(n):
    return isinstance(n, int)


def macaron(nc, x_in, consts_in, cols_in, rows_in, bonus_in, weights_in, gate_in, wg_in, wu_in, wd_in, out):
    with ExitStack() as ctx:
        def sb(name, shape, dt=F32):
            return ctx.enter_context(nc.sbuf_tensor(name, shape, dt))

        def sem(name):
            return ctx.enter_context(nc.semaphore(name))

        bank = [ctx.enter_context(nc.psum_tensor(f"bank{i}", [P, 512], F32)) for i in range(8)]

        X = sb("X", [P, HALVES * T, C])
        H = sb("H", [P, HALVES * T, C])
        consts = sb("consts", [P, NCONST])
        cols = sb("cols", [P, len(COLS)])
        rows = sb("rows", [P, len(ROWS), C])
        bonus = sb("bonus", [P, HEADS])
        weights = sb("weights", [P, len(WEIGHTS), C])
        gate = sb("gate", [P, E])
        wg = sb("wg", [P, E * INTER])
        wu = sb("wu", [P, E * INTER])
        wd = sb("wd", [P, E * INTER])

        def const(name):
            a, b = CONST[name]
            return consts[:, a:b]

        def col(name):
            i = COLS.index(name)
            return cols[:, i:i + 1]

        def row(name):
            return rows[:, ROWS.index(name), :]

        def weight(name):
            return weights[:, WEIGHTS.index(name), :]

        ident = const("ident")

        mv = sb("mv", [P, 2, GROUP, 2])
        bn = sb("bn", [P, GROUP, 6])
        var2 = sb("var2", [P, 2, 2, GROUP])
        root = sb("root", [P, 2, 2, GROUP])
        rstd = sb("rstd", [P, 2, 2, GROUP])
        mv2 = sb("mv2", [P, 2, GROUP, 2])
        root2 = sb("root2", [P, 2, GROUP])
        rstd2 = sb("rstd2", [P, 2, GROUP])
        n1 = sb("n1", [P, 2, GROUP, C])
        n2 = sb("n2", [P, HALVES, T, C])
        n2T = sb("n2T", [P, 2, GROUP * P])
        L = sb("L", [P, T, E])
        L2 = sb("L2", [P, T, E])
        eq = sb("eq", [P, T, E])
        pick = sb("pick", [P, TOP, T, E])
        both = sb("both", [P, T, E])
        best = sb("best", [P, TOP, T])
        first = sb("first", [P, T])
        gap2 = sb("gap2", [P, T])
        wexp = sb("wexp", [P, T])
        wden = sb("wden", [P, T])
        share = sb("share", [P, HALVES, TOP, T])
        counts = sb("counts", [P, E, T])
        cum = sb("cum", [P, E, T])
        ones_et = sb("ones_et", [P, E, T])
        over = sb("over", [P, E, T])
        tiles_e = sb("tiles_e", [P, E])
        ends = sb("ends", [P, E])
        start = sb("start", [P, E])
        slot_e = sb("slot_e", [P, T, E])
        slot_f = sb("slot_f", [P, TOP, T])
        slot = sb("slot", [P, HALVES, TOP, T], I32)
        done_e = sb("done_e", [P, XT + 1, E])
        tile_ef = sb("tile_ef", [P, XT + 1])
        tile_e = sb("tile_e", [P, HALVES, XT + 1], I32)
        xs = sb("xs", [P, 4, C])
        xsT = sb("xsT", [P, 2, P])
        shared = sb("shared", [P, 2 * HEADS * P])
        sg, hid, hidT, n1T = (shared[:, i * 2 * INTER:(i + 1) * 2 * INTER].rearrange("p (b i) -> p b i", b=2)
                         for i in range(4))
        att = shared[:].rearrange("p (b h i) -> p b h i", b=2, h=HEADS)
        ys = sb("ys", [P, 4, C])
        Y = sb("Y", [P, TOP, T, C])
        zero = Y[:, 0, 0:SLOTS // FILL // P, :]

        wm = sb("wm", [P, HEADS, P])
        negd_col = sb("negd_col", [P, 1])
        expd_col = sb("expd_col", [P, 1])
        expd_row = sb("expd_row", [P, C])
        negd_row = sb("negd_row", [P, C])
        w_chunk = sb("w_chunk", [P, 1])
        w_since = sb("w_since", [P, P])
        w_until = sb("w_until", [P, C])
        amv = sb("amv", [P, T, 2])
        abn = sb("abn", [P, T, 6])
        aroot = sb("aroot", [P, T])
        arstd = sb("arstd", [P, T])
        xn = sb("xn", [P, 2, AG, C])
        xT = sb("xT", [P, 2, AT + 1])
        delta = sb("delta", [P, AT])
        mix = sb("mix", [P, 4, AT])
        rk = sb("rk", [P, 2, 2, AT])
        rx = sb("rx", [P, 2, AG, HQ, P])
        rw = sb("rw", [P, 2, AG, P])
        kw = sb("kw", [P, 2, AG, C])
        vn = sb("vn", [P, 2, AG, C])
        gn = sb("gn", [P, 2, AG, C])
        state = sb("state", [P, 2, C])
        add = sb("add", [P, C])
        y8 = sb("y8", [P, 2, AG, C])
        ysum = sb("ysum", [P, AG * HEADS])
        yc = sb("yc", [P, AG, C])
        sq = sb("sq", [P, AG, C])
        vsum = sb("vsum", [P, AG * HEADS])
        yroot = sb("yroot", [P, AG * HEADS])
        yrstd = sb("yrstd", [P, AG * HEADS])
        z = sb("z", [P, AG, C])
        zT = sb("zT", [P, AT])

        slot_rows = [nc.dram_tensor(f"slot_rows{h}", (SLOTS, C), F32, kind="Internal").ap() for h in range(HALVES)]
        y_rows = [nc.dram_tensor(f"y_rows{h}", (SLOTS, C), F32, kind="Internal").ap() for h in range(HALVES)]

        s_x = [sem(f"x_loaded{g}") for g in range(HALVES * G)]
        s_small = sem("small_loaded")
        s_big = sem("expert_weights_loaded")
        s_zero = sem("zero_ready")
        s_filled = sem("slots_filled")
        s_dve = sem("vector_step")
        s_var = sem("variances")
        s_root = sem("roots")
        s_n1 = sem("n1_ready")
        s_n1p = sem("n1_transposed")
        s_n1T = sem("n1T_ready")
        s_proj = sem("proj_done")
        s_var2 = sem("variances2")
        s_root2 = sem("roots2")
        s_n2 = sem("n2_ready")
        s_n2p = sem("n2_transposed")
        s_n2T = sem("n2T_ready")
        s_logit = sem("logits_done")
        s_logc = sem("logits_copied")
        s_gap = sem("top_gap_ready")
        s_exp = sem("top_exp_ready")
        s_pick = sem("picks_ready")
        s_count = sem("counts_done")
        s_table = sem("slots_ready")
        s_scat = [sem(f"rows_scattered{h}") for h in range(HALVES)]
        s_load = [sem(f"slot_rows_loaded{k}") for k in range(4)]
        s_xp = sem("xs_transposed")
        s_xT = sem("xsT_ready")
        s_gu = sem("gate_up_done")
        s_sg = sem("silu_ready")
        s_hid = sem("hidden_ready")
        s_hp = sem("hidden_transposed")
        s_hT = sem("hiddenT_ready")
        s_y = sem("down_done")
        s_yc = sem("y_copied")
        s_store = [sem(f"y_stored{k}") for k in range(4)]
        s_got = [sem(f"y_gathered{g}") for g in range(G)]
        s_comb = sem("combined")
        s_out = sem("output_stored")

        s_tab = sem("decay_tables_step")
        s_tabv = sem("decay_tables_ready")
        s_avar = sem("attn_variances")
        s_aroot = sem("attn_roots")
        s_xn = sem("xn_ready")
        s_xnp = sem("xn_transposed")
        s_XT = sem("XT_ready")
        s_delta = sem("delta_ready")
        s_mix = sem("mix_ready")
        s_rkp = sem("rk_projected")
        s_rk = sem("rk_ready")
        s_vgp = sem("vg_projected")
        s_vg = sem("vg_ready")
        s_kp = sem("k_rows_projected")
        s_kw = sem("kw_ready")
        s_rx = sem("rx_ready")
        s_sc = sem("scores_done")
        s_att = sem("att_ready")
        s_kv = sem("kv_done")
        s_add = sem("kv_masked")
        s_state = sem("state_ready")
        s_av = sem("chunk_output_done")
        s_y8 = sem("chunk_output_copied")
        s_ysum = sem("head_sums")
        s_ycen = sem("centred")
        s_sq = sem("squared")
        s_vsum = sem("head_square_sums")
        s_yvar = sem("head_variances")
        s_yroot = sem("head_roots")
        s_gn = sem("group_norm_step")
        s_z = sem("z_ready")
        s_zp = sem("z_transposed")
        s_zT = sem("zT_ready")
        s_o = sem("attn_out_done")
        s_xa = sem("attn_added")

        block = ctx.enter_context(nc.Block())
        RUNS = [(0, 0), (0, 1), (1, 0), (1, 1)]
        NXT = XT

        LO, HI, UN = 3, 35, 4

        @block.sync
        def _(sp):
            sp.dma_start(consts[:], consts_in).then_inc(s_small, 16)
            sp.dma_start(cols[:], cols_in).then_inc(s_small, 16)
            sp.dma_start(weights[:], weights_in).then_inc(s_small, 16)
            sp.dma_start(gate[:], gate_in).then_inc(s_small, 16)
            sp.dma_start(rows[:], rows_in).then_inc(s_small, 16)
            sp.dma_start(bonus[:], bonus_in).then_inc(s_small, 16)
            for g in range(HALVES * G):
                sp.dma_start(X[:, g * GROUP:(g + 1) * GROUP, :],
                             x_in[g * GROUP * P:(g + 1) * GROUP * P, :].rearrange("(t p) c -> p t c", p=P)
                             ).then_inc(s_x[g], 16)
            sp.wait_ge(s_zero, 1)
            for h in range(HALVES):
                for q in range(FILL):
                    n = SLOTS // FILL
                    sp.dma_start(slot_rows[h][q * n:(q + 1) * n, :].rearrange("(p a) c -> p a c", p=P),
                                 zero).then_inc(s_filled, 16)
            for dst, src in ((wg, wg_in), (wu, wu_in), (wd, wd_in)):
                sp.dma_start(dst[:], src).then_inc(s_big, 16)

            for run, (layer, half) in enumerate(RUNS):
                base = run * NXT
                sp.wait_ge(s_scat[half], 16 * TOP * T * (layer + 1))

                def load(n, k):
                    if not known(n) or base + n >= 4:
                        sp.wait_ge(s_xp, n + (base - 3))
                    sp.dma_start(xs[:, k, :], slot_rows[half][bass.ds(n * P, P), :]).then_inc(s_load[k], 16)

                def store(n, k):
                    sp.wait_ge(s_yc, n + (base + 1))
                    sp.dma_start(y_rows[half][bass.ds(n * P, P), :], ys[:, k, :]).then_inc(s_store[k], 16)

                def step(n, k):
                    if not known(n) or n < NXT:
                        load(n, (base + k) % 4)
                    if not known(n) or n >= 5:
                        store(n - 5, (base + k - 5) % 4)

                steps(sp, 0, 5, 37, NXT + 4, 4, step)
            for half in range(HALVES):
                for g in range(G):
                    sp.wait_ge(s_comb, (2 + half) * G + g + 1)
                    t = half * T + g * GROUP
                    sp.dma_start(out[t * P:(t + GROUP) * P, :].rearrange("(t p) c -> p t c", p=P),
                                 X[:, t:t + GROUP, :]).then_inc(s_out, 16)
            sp.wait_ge(s_out, 16 * HALVES * G)

        @block.gpsimd
        def _(pool):
            pool.memset(zero, 0.0).then_inc(s_zero, 1)

            def scatter(run):
                layer, half = RUNS[run]
                if layer == 0:
                    pool.wait_ge(s_filled, 16 * FILL * HALVES)
                pool.wait_ge(s_table, run + 1)
                for t in range(T):
                    for k in range(TOP):
                        pool.indirect_dma_start(
                            slot_rows[half], bass.IndirectOffsetOnAxis(slot[:, half, k, t:t + 1], 0),
                            n2[:, half, t, :], None).then_inc(s_scat[half], 16)

            def gather(run):
                layer, half = RUNS[run]
                for k in range(4):
                    pool.wait_ge(s_store[k], 16 * len([n for n in range((run + 1) * NXT) if n % 4 == k]))
                if run:
                    pool.wait_ge(s_comb, run * G)
                for t in range(T):
                    for k in range(TOP):
                        pool.indirect_dma_start(
                            Y[:, k, t, :], None, y_rows[half],
                            bass.IndirectOffsetOnAxis(slot[:, half, k, t:t + 1], 0)
                        ).then_inc(s_got[t // GROUP], 16)

            scatter(0)
            scatter(1)
            gather(0)
            gather(1)
            scatter(2)
            scatter(3)
            gather(2)
            gather(3)

        @block.scalar
        def _(act):
            def front(run):
                def step(s):
                    n = run * G + s
                    if 0 <= s < G:
                        act.wait_ge(s_var, n + 1)
                        act.activation(root[:, n % 2], var2[:, n % 2], ACT.Sqrt).then_inc(s_root, 1)
                    if 0 <= s - 1 < G:
                        m = n - 1
                        act.wait_ge(s_n1p, m + 1)
                        act.activation(n1T[:, m % 2, :], bank[m % 2][:], ACT.Identity,
                                       bias=col("ln1_b"), scale=col("ln1_g")).then_inc(s_n1T, 1)
                    if 0 <= s - 2 < G:
                        m = n - 2
                        act.wait_ge(s_var2, m + 1)
                        act.activation(root2[:, m % 2], mv2[:, m % 2, :, 1], ACT.Sqrt).then_inc(s_root2, 1)
                    if 0 <= s - 3 < G:
                        m = n - 3
                        act.wait_ge(s_n2p, m + 1)
                        act.activation(n2T[:, m % 2, :], bank[4 + m % 2][:], ACT.Identity,
                                       bias=col("ln2_b"), scale=col("ln2_g")).then_inc(s_n2T, 1)
                for s in range(G + 4):
                    step(s)
                act.wait_ge(s_gap, run + 1)
                act.activation(wexp[:], gap2[:], ACT.Exp).then_inc(s_exp, 1)

            def experts(run):
                base = run * NXT

                def step(n, k):
                    k2 = (base + k) % 2
                    if not known(n) or n + 1 < NXT:
                        act.wait_ge(s_xp, n + (base + 2))
                        act.activation(xsT[:, 1 - k2, :], bank[0][:, 0:P], ACT.Identity,
                                       bias=col("ln2_b"), scale=col("ln2_g")).then_inc(s_xT, 1)
                    if not known(n) or 0 <= n < NXT:
                        act.wait_ge(s_gu, n + (base + 1))
                        act.activation(sg[:, k2, :], bank[1 + k2][:], ACT.Silu).then_inc(s_sg, 1)
                    if not known(n) or 1 <= n < NXT + 1:
                        act.wait_ge(s_hp, n + base)
                        act.activation(hidT[:, 1 - k2, :], bank[5 + (1 - k2)][:], ACT.Copy).then_inc(s_hT, 1)

                steps(act, -1, LO, HI, NXT, UN, step)

            def tables():
                act.activation(expd_col[:], col("decay"), ACT.Exp)
                act.activation(expd_row[:], row("decay"), ACT.Exp).then_inc(s_tab, 1)
                act.wait_ge(s_tabv, 1)
                act.activation(w_chunk[:], negd_col[:], ACT.Exp, scale=float(P))
                act.activation(w_since[:], const("iota"), ACT.Exp, scale=negd_col[:])
                act.activation(w_until[:], negd_row[:], ACT.Exp, scale=const("left"))
                for h in range(HEADS):
                    ins = act.activation(wm[:, h, :], const("gap"), ACT.Exp, scale=negd_row[:, h * HD:h * HD + 1])
                ins.then_inc(s_tab, 1)

            def attention(half):
                B = half * NQ
                act.wait_ge(s_avar, half + 1)
                act.activation(aroot[:], amv[:, :, 1], ACT.Sqrt).then_inc(s_aroot, 1)

                def step(n, p):
                    if not known(n) or n + 1 < NQ:
                        q = 1 - p
                        act.wait_ge(s_xnp, n + (B + 2))
                        if known(n) and n == -1:
                            act.activation(xT[:, q, 0:1], consts[:, 0:1], ACT.Copy, scale=0.0)
                        else:
                            act.wait_ge(s_XT, n + (B + 1))
                            if known(n) and n == 0:
                                pass
                            act.activation(xT[:, q, 0:1], xT[:, p, AT:AT + 1], ACT.Copy)
                        act.activation(xT[:, q, 1:AT + 1], bank[6][:, 0:AT], ACT.Copy).then_inc(s_XT, 1)
                    if not known(n) or 1 <= n <= NQ:
                        act.wait_ge(s_ycen, n + B)
                        act.activation(sq[:], yc[:], ACT.Square).then_inc(s_sq, 1)
                    if not known(n) or 0 <= n < NQ:
                        act.wait_ge(s_av, n * 2 + (2 * B + 1))
                        if not known(n) or n >= 2:
                            act.wait_ge(s_ycen, n + (B - 1))
                        act.activation(y8[:, p, 0, :], bank[4][:, 0:C], ACT.Copy, scale=1.0 / HD).then_inc(s_y8, 1)
                    if not known(n) or 1 <= n <= NQ:
                        act.wait_ge(s_yvar, n + B)
                        act.activation(yroot[:], vsum[:], ACT.Sqrt).then_inc(s_yroot, 1)
                    if not known(n) or n + 1 < NQ:
                        q = 1 - p
                        act.wait_ge(s_rkp, n + (B + 2))
                        act.activation(rk[:, q].rearrange("p a t -> p (a t)"), bank[7][:], ACT.Copy).then_inc(s_rk, 1)
                        act.wait_ge(s_vgp, n + (B + 2))
                        if not known(n) or n >= 1:
                            act.wait_ge(s_z, n + B)
                        act.activation(vn[:, q], bank[6][:, 0:AT].rearrange("p (a c) -> p a c", a=AG), ACT.Copy)
                        act.activation(gn[:, q], bank[6][:, AT:2 * AT].rearrange("p (a c) -> p a c", a=AG),
                                       ACT.Silu).then_inc(s_vg, 1)
                    if not known(n) or 1 <= n <= NQ:
                        act.wait_ge(s_zp, n + B)
                        act.activation(zT[:], bank[6][:, 0:AT], ACT.Copy).then_inc(s_zT, 1)
                    if not known(n) or 0 <= n < NQ:
                        act.wait_ge(s_av, n * 2 + (2 * B + 2))
                        act.activation(y8[:, p, 1, :], bank[4][:, 0:C], ACT.Copy, scale=1.0 / HD).then_inc(s_y8, 1)

                steps(act, -1, 2, 6, NQ, 2, step)

            act.wait_ge(s_small, 16 * 6)
            front(0)
            front(1)
            tables()
            experts(0)
            experts(1)
            attention(0)
            front(2)
            attention(1)
            front(3)
            experts(2)
            experts(3)

        def stored(n, k, base):
            rest = (base + k - 2) % 4
            if known(n):
                return 16 * ((base + n - 2) // 4)
            return n * 4 + (4 * (base - 2 - rest))

        @block.vector
        def _(dve):
            link = Chain(dve, s_dve)

            def norm_stats(run, s):
                n = run * G + s
                par = n % 2
                t0 = RUNS[run][1] * T + s * GROUP
                if run == 0 or run == 1:
                    dve.wait_ge(s_x[run * G + s], 16)
                for t in range(GROUP):
                    link.step(dve.bn_stats(bn[:, t, :], X[:, t0 + t, :]))
                for t in range(GROUP):
                    link.wait()
                    link.step(dve.bn_aggr(mv[:, par, t, :], bn[:, t, :]))
                link.wait()
                link.step(dve.tensor_scalar(var2[:, par, 0, :], mv[:, par, :, 1], EPS, None, ALU.add))
                dve.tensor_scalar(var2[:, par, 1, :], mv[:, par, :, 1], 1.0 + EPS, EPS * EPS,
                                  ALU.mult, ALU.add).then_inc(s_var, 1)
                link.wait()

            def norm_apply(run, s):
                n = run * G + s
                par = n % 2
                t0 = RUNS[run][1] * T + s * GROUP
                dve.wait_ge(s_root, n + 1)
                link.step(dve.reciprocal(rstd[:, par], root[:, par]))
                link.wait()
                if n >= 2:
                    dve.wait_ge(s_n1p, n - 1)
                for t in range(GROUP):
                    ins = dve.tensor_scalar(n1[:, par, t, :], X[:, t0 + t, :], mv[:, par, t, 0:1],
                                            rstd[:, par, 1, t:t + 1], ALU.subtract, ALU.mult)
                ins.then_inc(s_n1, 1)
                for t in range(GROUP):
                    link.step(dve.tensor_scalar(H[:, t0 + t, :], X[:, t0 + t, :], mv[:, par, t, 0:1],
                                                rstd[:, par, 0, t:t + 1], ALU.subtract, ALU.mult))

            def add_proj(run, s):
                n = run * G + s
                par = n % 2
                t0 = RUNS[run][1] * T + s * GROUP
                dve.wait_ge(s_proj, n + 1)
                link.wait()
                hg = H[:, t0:t0 + GROUP, :]
                link.step(dve.tensor_tensor(hg, hg, bank[2 + par][:].rearrange("p (t c) -> p t c", c=C), ALU.add))
                link.wait()
                for t in range(GROUP):
                    link.step(dve.bn_stats(bn[:, t, :], H[:, t0 + t, :]))
                for t in range(GROUP):
                    link.wait()
                    link.step(dve.bn_aggr(mv2[:, par, t, :], bn[:, t, :]))
                link.wait()
                dve.tensor_scalar(mv2[:, par, :, 1], mv2[:, par, :, 1], EPS, None, ALU.add).then_inc(s_var2, 1)

            def norm2_apply(run, s):
                n = run * G + s
                par = n % 2
                layer, half = RUNS[run]
                t0 = half * T + s * GROUP
                dve.wait_ge(s_root2, n + 1)
                link.step(dve.reciprocal(rstd2[:, par], root2[:, par]))
                link.wait()
                if layer and s == 0:
                    dve.wait_ge(s_scat[half], 16 * TOP * T * layer)
                for t in range(GROUP):
                    ins = dve.tensor_scalar(n2[:, half, s * GROUP + t, :], H[:, t0 + t, :], mv2[:, par, t, 0:1],
                                            rstd2[:, par, t:t + 1], ALU.subtract, ALU.mult)
                ins.then_inc(s_n2, 1)

            def logits(run, s):
                n = run * G + s
                dve.wait_ge(s_logit, n + 1)
                dve.tensor_copy(L[:, s * GROUP:(s + 1) * GROUP, :],
                                bank[6][:, 0:GROUP * E].rearrange("p (t e) -> p t e", e=E)).then_inc(s_logc, 1)

            def per_tile(v):
                return v.unsqueeze(2).broadcast_to([P, T, E])

            def per_expert(v, n=T):
                return v.unsqueeze(1).broadcast_to([P, n, E])

            def route(run):
                layer, half = RUNS[run]
                rank = per_expert(const("rank"))
                dve.wait_ge(s_logc, (run + 1) * G)
                src = L
                for k in range(TOP):
                    link.step(dve.tensor_reduce(best[:, k], src[:], AX, ALU.max))
                    link.wait()
                    link.step(dve.tensor_tensor(eq[:], src[:], per_tile(best[:, k]), ALU.is_equal))
                    link.wait()
                    link.step(dve.tensor_tensor(eq[:], eq[:], rank, ALU.mult))
                    link.wait()
                    link.step(dve.tensor_reduce(first[:], eq[:], AX, ALU.max))
                    link.wait()
                    link.step(dve.tensor_tensor(pick[:, k], rank, per_tile(first[:]), ALU.is_equal))
                    link.wait()
                    if k == 0:
                        link.step(dve.scalar_tensor_tensor(L2[:], pick[:, 0], -BIG, L[:], ALU.mult, ALU.add))
                        link.wait()
                        src = L2
                dve.tensor_tensor(gap2[:], best[:, 1], best[:, 0], ALU.subtract).then_inc(s_gap, 1)
                dve.tensor_tensor(both[:], pick[:, 0], pick[:, 1], ALU.add).then_inc(s_pick, 1)
                dve.wait_ge(s_exp, run + 1)
                link.step(dve.tensor_scalar(wden[:], wexp[:], 1.0, 2.0, ALU.add, ALU.mult))
                link.wait()
                link.step(dve.reciprocal(share[:, half, 0], wden[:]))
                link.wait()
                link.step(dve.tensor_tensor(share[:, half, 1], share[:, half, 0], wexp[:], ALU.mult))
                dve.wait_ge(s_count, run + 1)
                before = bank[7][:, 0:T * E].rearrange("p (t e) -> p t e", e=E)
                whole = bank[7][:, T * E:2 * T * E].rearrange("p (t e) -> p e t", e=E)
                link.step(dve.tensor_copy(counts[:], whole))
                link.wait()
                ones = ones_et[:].rearrange("p e t -> p (e t)")
                link.step(dve.tensor_tensor_scan(cum[:].rearrange("p e t -> p (e t)"), ones,
                                                 counts[:].rearrange("p e t -> p (e t)"), 0.0, ALU.mult, ALU.add))
                link.wait()
                link.step(dve.tensor_tensor(over[:], cum[:, :, T - 1:T].broadcast_to([P, E, T]),
                                            const("limit").unsqueeze(1).broadcast_to([P, E, T]), ALU.is_gt))
                link.wait()
                link.step(dve.tensor_reduce(tiles_e[:], over[:], AX, ALU.add))
                link.wait()
                link.step(dve.tensor_tensor_scan(ends[:], const("ones")[:, 0:E], tiles_e[:], 0.0, ALU.mult, ALU.add))
                link.wait()
                link.step(dve.tensor_tensor(start[:], ends[:], tiles_e[:], ALU.subtract))
                link.wait()
                link.step(dve.tensor_tensor(cum[:], cum[:], counts[:], ALU.subtract))
                link.wait()
                link.step(dve.tensor_tensor(slot_e[:], cum[:].rearrange("p e t -> p t e"), before, ALU.add))
                link.wait()
                link.step(dve.scalar_tensor_tensor(slot_e[:], per_expert(start[:]), float(P), slot_e[:],
                                                   ALU.mult, ALU.add))
                for k in range(TOP):
                    link.wait()
                    link.step(dve.tensor_tensor(eq[:], slot_e[:], pick[:, k], ALU.mult))
                    link.wait()
                    link.step(dve.tensor_reduce(slot_f[:, k], eq[:], AX, ALU.add))
                n = XT + 1
                link.step(dve.tensor_tensor(done_e[:], per_expert(ends[:], n),
                                            const("tile").unsqueeze(2).broadcast_to([P, n, E]), ALU.is_le))
                link.wait()
                link.step(dve.tensor_reduce(tile_ef[:], done_e[:], AX, ALU.add))
                link.wait()
                link.step(dve.tensor_scalar(tile_e[:, half], tile_ef[:], float(E - 1), float(INTER),
                                            ALU.min, ALU.mult))
                link.wait()
                dve.tensor_copy(slot[:, half], slot_f[:]).then_inc(s_table, 1)

            def front(run):
                for s in range(G + 4):
                    if s < G:
                        norm_stats(run, s)
                    if 0 <= s - 1 < G:
                        norm_apply(run, s - 1)
                    if 0 <= s - 2 < G:
                        add_proj(run, s - 2)
                    if 0 <= s - 3 < G:
                        norm2_apply(run, s - 3)
                    if 0 <= s - 4 < G:
                        logits(run, s - 4)
                route(run)

            def experts(run):
                base = run * NXT

                def step(n, k):
                    k2 = (base + k) % 2
                    if not known(n) or n < NXT:
                        dve.wait_ge(s_sg, n + (base + 1))
                        dve.tensor_tensor(hid[:, k2, :], sg[:, k2, :], bank[3 + k2][:],
                                          ALU.mult).then_inc(s_hid, 1)
                    if not known(n) or n >= 2:
                        j = (base + k - 2) % 4
                        dve.wait_ge(s_y, n + (base - 1))
                        if not known(n) or base + n - 2 >= 4:
                            dve.wait_ge(s_store[j], stored(n, k, base))
                        dve.tensor_copy(ys[:, j, :], bank[7][:, 0:C]).then_inc(s_yc, 1)

                steps(dve, 0, LO, HI, NXT + 1, UN, step)

            def combine(run):
                layer, half = RUNS[run]
                for g in range(G):
                    t0 = half * T + g * GROUP
                    dve.wait_ge(s_got[g], 16 * GROUP * TOP * (run + 1))
                    xg = X[:, t0:t0 + GROUP, :]
                    link.step(dve.scalar_tensor_tensor(xg, H[:, t0:t0 + GROUP, :], 0.5, xg, ALU.mult, ALU.add))
                    link.wait()
                    for k in range(TOP):
                        for t in range(GROUP):
                            ins = dve.scalar_tensor_tensor(
                                X[:, t0 + t, :], Y[:, k, g * GROUP + t, :], share[:, half, k, g * GROUP + t:g * GROUP + t + 1],
                                X[:, t0 + t, :], ALU.mult, ALU.add)
                            if k == 0:
                                link.step(ins)
                        if k == 0:
                            link.wait()
                    ins.then_inc(s_comb, 1)

            def tables():
                dve.wait_ge(s_tab, 1)
                dve.tensor_scalar(negd_col[:], expd_col[:], DECAY_MAX, -1.0, ALU.min, ALU.mult)
                dve.tensor_scalar(negd_row[:], expd_row[:], DECAY_MAX, -1.0, ALU.min, ALU.mult).then_inc(s_tabv, 1)
                dve.wait_ge(s_tab, 2)
                link.step(dve.tensor_tensor(wm[:], wm[:], const("later").unsqueeze(1).broadcast_to([P, HEADS, P]),
                                            ALU.mult))
                link.wait()
                for h in range(HEADS):
                    link.step(dve.scalar_tensor_tensor(wm[:, h, :], ident, bonus[:, h:h + 1], wm[:, h, :],
                                                       ALU.mult, ALU.add))

            def attn_stats(half):
                link.wait()
                for t in range(T):
                    link.step(dve.bn_stats(abn[:, t, :], X[:, half * T + t, :]))
                link.wait()
                for t in range(T):
                    link.step(dve.bn_aggr(amv[:, t, :], abn[:, t, :]))
                link.wait()
                dve.tensor_scalar(amv[:, :, 1], amv[:, :, 1], EPS, None, ALU.add).then_inc(s_avar, 1)
                link.step(dve.memset(state[:, 0, :], 0.0))
                dve.wait_ge(s_aroot, half + 1)
                link.step(dve.reciprocal(arstd[:], aroot[:]))
                link.wait()

            def attention(half):
                B = half * NQ
                dve.wait_ge(s_comb, (half + 1) * G)
                attn_stats(half)

                def mask(n, p, c):
                    if not known(n) or n >= 1:
                        dve.wait_ge(s_av, n * 2 + (2 * B - 1 + c))
                    for q in range(4):
                        dve.wait_ge(s_sc, n * 8 + (8 * B + 4 * c + q + 1))
                        dve.tensor_tensor(att[:, c, 4 * q:4 * q + 4, :],
                                          bank[q][:].rearrange("p (h i) -> p h i", i=P),
                                          wm[:, 4 * q:4 * q + 4, :], ALU.mult).then_inc(s_att, 1)

                def update(n, c):
                    dve.wait_ge(s_kv, n * 2 + (2 * B + c + 1))
                    if c == 1 or not known(n) or n >= 1:
                        dve.wait_ge(s_state, n * 2 + (2 * B + c))
                    dve.tensor_tensor(add[:], bank[5][:, 0:C], const("block"), ALU.mult).then_inc(s_add, 1)
                    dve.wait_ge(s_add, n * 2 + (2 * B + c + 1))
                    if c == 1 or not known(n) or n >= 1:
                        dve.wait_ge(s_av, n * 2 + (2 * B + c))
                    dve.scalar_tensor_tensor(state[:, 1 - c, :], state[:, c, :], w_chunk[:], add[:],
                                             ALU.mult, ALU.add).then_inc(s_state, 1)

                def step(n, p):
                    prep = not known(n) or n + 1 < NQ
                    core = not known(n) or 0 <= n < NQ
                    close = not known(n) or 1 <= n <= NQ
                    q = 1 - p
                    t1 = n * AG + (half * T + AG)
                    if prep:
                        if not known(n) or n >= 1:
                            dve.wait_ge(s_xnp, n + B)
                        for a in range(AG):
                            if known(n):
                                tt = (n + 1) * AG + a
                            ins = dve.tensor_scalar(
                                xn[:, q, a, :], X[:, half * T + tt, :] if known(n) else X[:, bass.ds(t1 + a, 1), :],
                                mean(n, a), rs(n, a), ALU.subtract, ALU.mult)
                        ins.then_inc(s_xn, 1)
                    if core:
                        mask(n, p, 0)
                    if close:
                        dve.wait_ge(s_y8, n * 2 + 2 * B)
                        dve.tensor_reduce(ysum[:], heads(y8[:, q]), AX, ALU.add).then_inc(s_ysum, 1)
                        dve.wait_ge(s_ysum, n + B)
                        if not known(n) or n >= 2:
                            dve.wait_ge(s_sq, n + (B - 1))
                        dve.scalar_tensor_tensor(heads(yc[:]), bc(ysum), -1.0 / HD, heads(y8[:, q]),
                                                 ALU.mult, ALU.add).then_inc(s_ycen, 1)
                    if not known(n) or n >= 2:
                        dve.wait_ge(s_o, n + (B - 1))
                        t0 = n * AG + (half * T - 2 * AG)
                        xg = X[:, bass.ds(t0, AG), :]
                        dve.tensor_tensor(xg, xg, bank[7][:, 0:AT].rearrange("p (a c) -> p a c", a=AG),
                                          ALU.add).then_inc(s_xa, 1)
                    if prep:
                        dve.wait_ge(s_XT, n + (B + 2))
                        dve.tensor_tensor(delta[:], xT[:, q, 1:AT + 1], xT[:, q, 0:AT], ALU.subtract).then_inc(s_delta, 1)
                        dve.wait_ge(s_delta, n + (B + 2))
                        if not known(n) or n + B >= 0:
                            dve.wait_ge(s_kp, n + (B + 1))
                        for i, m in enumerate("rkvg"):
                            ins = dve.scalar_tensor_tensor(mix[:, i, :], delta[:], col("mix_" + m), xT[:, q, 0:AT],
                                                           ALU.mult, ALU.add)
                        ins.then_inc(s_mix, 1)
                    if core:
                        update(n, 0)
                    if close:
                        dve.wait_ge(s_sq, n + B)
                        dve.tensor_reduce(vsum[:], heads(sq[:]), AX, ALU.add).then_inc(s_vsum, 1)
                        dve.wait_ge(s_vsum, n + B)
                        dve.tensor_scalar(vsum[:], vsum[:], 1.0 / HD, EPS, ALU.mult, ALU.add).then_inc(s_yvar, 1)
                    if core:
                        mask(n, p, 1)
                    if prep:
                        dve.wait_ge(s_rk, n + (B + 2))
                        r = rk[:, q, 0, :].rearrange("p (a t) -> p a t", a=AG)
                        for l in range(HQ):
                            dve.tensor_scalar(rx[:, q, :, l, :], r, const("heads4")[:, l:l + 1], None, ALU.mult)
                        dve.tensor_tensor(rw[:, q], r, w_since[:].unsqueeze(1).broadcast_to([P, AG, P]),
                                          ALU.mult).then_inc(s_rx, 1)
                        dve.wait_ge(s_kp, n + (B + 2))
                        dve.tensor_tensor(kw[:, q], bank[7][:, 0:AT].rearrange("p (a c) -> p a c", a=AG),
                                          w_until[:].unsqueeze(1).broadcast_to([P, AG, C]), ALU.mult).then_inc(s_kw, 1)
                    if close:
                        dve.wait_ge(s_yroot, n + B)
                        dve.reciprocal(yrstd[:], yroot[:]).then_inc(s_gn, 1)
                        dve.wait_ge(s_gn, n * 4 + (4 * B - 3))
                        if not known(n) or n + B >= 2:
                            dve.wait_ge(s_zp, n + (B - 1))
                        dve.tensor_tensor(heads(z[:]), heads(yc[:]), bc(yrstd), ALU.mult).then_inc(s_gn, 1)
                        dve.wait_ge(s_gn, n * 4 + (4 * B - 2))
                        dve.tensor_tensor(z[:], z[:], row("ln_w").unsqueeze(1).broadcast_to([P, AG, C]),
                                          ALU.mult).then_inc(s_gn, 1)
                        dve.wait_ge(s_gn, n * 4 + (4 * B - 1))
                        dve.tensor_tensor(z[:], z[:], row("ln_b").unsqueeze(1).broadcast_to([P, AG, C]),
                                          ALU.add).then_inc(s_gn, 1)
                        dve.wait_ge(s_gn, n * 4 + 4 * B)
                        dve.wait_ge(s_vg, n + B)
                        dve.tensor_tensor(z[:], z[:], gn[:, q], ALU.mult).then_inc(s_z, 1)
                    if core:
                        update(n, 1)

                def heads(v):
                    return v.rearrange("p a (h d) -> p (a h) d", d=HD)

                def bc(v):
                    return v[:].unsqueeze(2).broadcast_to([P, AG * HEADS, HD])

                def mean(n, a):
                    return amv[:, bass.ds(n * AG + (AG + a), 1), 0]

                def rs(n, a):
                    return arstd[:, bass.ds(n * AG + (AG + a), 1)]

                steps(dve, -1, 2, 6, NQ + 1, 2, step)

            link.step(dve.memset(ones_et[:], 1.0))
            link.wait()
            link.step(dve.memset(ones_et[:, :, 0:1], 0.0))
            dve.wait_ge(s_small, 16 * 6)
            front(0)
            front(1)
            tables()
            experts(0)
            experts(1)
            combine(0)
            attention(0)
            combine(1)
            front(2)
            attention(1)
            front(3)
            experts(2)
            experts(3)
            combine(2)
            combine(3)

        @block.tensor
        def _(pe):
            def front(run):
                layer, half = RUNS[run]
                for s in range(1, G + 4):
                    n = run * G + s
                    if 0 <= s - 1 < G:
                        m = n - 1
                        pe.wait_ge(s_n1, m + 1)
                        if m >= 2:
                            pe.wait_ge(s_n1T, m - 1)
                        for t in range(GROUP):
                            mm = pe.transpose(bank[m % 2][:, t * P:(t + 1) * P], n1[:, m % 2, t, :], ident)
                        mm.then_inc(s_n1p, 1)
                    if 0 <= s - 2 < G:
                        m = n - 2
                        pe.wait_ge(s_n1T, m + 1)
                        if m >= 2:
                            pe.wait_ge(s_var2, m - 1)
                        for t in range(GROUP):
                            mm = pe.matmul(bank[2 + m % 2][:, t * C:(t + 1) * C], n1T[:, m % 2, t * P:(t + 1) * P],
                                           weight("proj"), start=True, stop=True)
                        mm.then_inc(s_proj, 1)
                    if 0 <= s - 3 < G:
                        m = n - 3
                        pe.wait_ge(s_n2, m + 1)
                        if m >= 2:
                            pe.wait_ge(s_n2T, m - 1)
                        for t in range(GROUP):
                            mm = pe.transpose(bank[4 + m % 2][:, t * P:(t + 1) * P],
                                              n2[:, half, (s - 3) * GROUP + t, :], ident)
                        mm.then_inc(s_n2p, 1)
                    if 0 <= s - 4 < G:
                        m = n - 4
                        pe.wait_ge(s_n2T, m + 1)
                        if m >= 1:
                            pe.wait_ge(s_logc, m)
                        for t in range(GROUP):
                            mm = pe.matmul(bank[6][:, t * E:(t + 1) * E], n2T[:, m % 2, t * P:(t + 1) * P],
                                           gate[:], start=True, stop=True)
                        mm.then_inc(s_logit, 1)
                pe.wait_ge(s_pick, run + 1)
                if run:
                    pe.wait_ge(s_table, run)
                flat = both[:].rearrange("p t e -> p (t e)")
                pe.matmul(bank[7][:, 0:T * E], const("before"), flat, start=True, stop=True)
                pe.matmul(bank[7][:, T * E:2 * T * E], const("ones"), flat, start=True, stop=True
                          ).then_inc(s_count, 1)

            def experts(run):
                layer, half = RUNS[run]
                base = run * NXT
                pe.wait_ge(s_table, run + 1)
                if run == 0:
                    pe.wait_ge(s_big, 16 * 3)

                def step(n, k):
                    k2 = (base + k) % 2
                    k4 = (base + k + 1) % 4
                    if not known(n) or n + 1 < NXT:
                        if known(n):
                            pe.wait_ge(s_load[k4], 16 * ((base + n + 1) // 4 + 1))
                        else:
                            pe.wait_ge(s_load[k4], n * 4 + (4 * (base + 1 - k4) + 16))
                        if not known(n) or n + base >= 0:
                            pe.wait_ge(s_xT, n + (base + 1))
                        pe.transpose(bank[0][:, 0:P], xs[:, k4, :], ident).then_inc(s_xp, 1)
                    if not known(n) or 0 <= n < NXT:
                        at = pe.value_load(tile_e[0:1, half, bass.ds(n, 1)], min_val=0, max_val=(E - 1) * INTER)
                        pe.wait_ge(s_xT, n + (base + 1))
                        if not known(n) or base + n >= 2:
                            pe.wait_ge(s_hid, n + (base - 1))
                        pe.matmul(bank[1 + k2][:], xsT[:, k2, :], wg[:, bass.ds(at, INTER)], start=True, stop=True)
                        pe.matmul(bank[3 + k2][:], xsT[:, k2, :], wu[:, bass.ds(at, INTER)], start=True, stop=True
                                  ).then_inc(s_gu, 1)
                    if not known(n) or 1 <= n < NXT + 1:
                        pe.wait_ge(s_hid, n + base)
                        if not known(n) or base + n - 1 >= 2:
                            pe.wait_ge(s_hT, n + (base - 2))
                        for c in range(CH):
                            mm = pe.transpose(bank[5 + (1 - k2)][:, c * P:(c + 1) * P],
                                              hid[:, 1 - k2, c * P:(c + 1) * P], ident)
                        mm.then_inc(s_hp, 1)
                    if not known(n) or 2 <= n < NXT + 2:
                        at = pe.value_load(tile_e[0:1, half, bass.ds(n - 2, 1)], min_val=0, max_val=(E - 1) * INTER)
                        pe.wait_ge(s_hT, n + (base - 1))
                        if not known(n) or base + n - 2 >= 1:
                            pe.wait_ge(s_yc, n + (base - 2))
                        for c in range(CH):
                            mm = pe.matmul(bank[7][:, 0:C], hidT[:, k2, c * P:(c + 1) * P],
                                           wd[:, bass.ds(at + c * P, C)], start=(c == 0), stop=(c == CH - 1))
                        mm.then_inc(s_y, 1)

                steps(pe, -1, LO, HI, NXT + 1, UN, step)

            def attention(half):
                B = half * NQ
                if half == 0:
                    pe.wait_ge(s_yc, 2 * NXT)
                else:
                    pe.wait_ge(s_table, 3)

                def scores(n, p, c):
                    for q in range(4):
                        if not known(n) or c or n >= 1:
                            pe.wait_ge(s_att, n * 8 + (8 * B + 4 * c + q - 3))
                        pe.matmul(bank[q][:], rk[32 * q:32 * q + 32, p, 1, c * P:(c + 1) * P],
                                  rx[32 * q:32 * q + 32, p, c].rearrange("p l i -> p (l i)"),
                                  start=True, stop=True).then_inc(s_sc, 1)

                def chunk_kv(n, p, c):
                    if not known(n) or c or n >= 1:
                        pe.wait_ge(s_add, n * 2 + (2 * B + c))
                    pe.matmul(bank[5][:, 0:C], kw[:, p, c, :], vn[:, p, c, :], start=True, stop=True
                              ).then_inc(s_kv, 1)

                def chunk_out(n, p, c):
                    if not known(n) or c or n >= 1:
                        pe.wait_ge(s_y8, n * 2 + (2 * B + c))
                        pe.wait_ge(s_state, n * 2 + (2 * B + c))
                    pe.matmul(bank[4][:, 0:C], rw[:, p, c, :], state[:, c, :], start=True, stop=False,
                              skip_group_check=True)
                    pe.wait_ge(s_att, n * 8 + (8 * B + 4 * c + 4))
                    for h in range(HEADS):
                        mm = pe.matmul(bank[4][:, h * HD:(h + 1) * HD], att[:, c, h, :],
                                       vn[:, p, c, h * HD:(h + 1) * HD], start=False, stop=(h == HEADS - 1),
                                       skip_group_check=True)
                    mm.then_inc(s_av, 1)

                def step(n, p):
                    prep = not known(n) or n + 1 < NQ
                    core = not known(n) or 0 <= n < NQ
                    close = not known(n) or 1 <= n <= NQ
                    q = 1 - p
                    if core:
                        pe.wait_ge(s_rx, n + (B + 1))
                        scores(n, p, 0)
                    if prep:
                        pe.wait_ge(s_xn, n + (B + 2))
                        if not known(n) or n >= 2:
                            pe.wait_ge(s_zT, n + (B - 1))
                        elif n >= 0:
                            pe.wait_ge(s_vg, n + (B + 1))
                        for a in range(AG):
                            mm = pe.transpose(bank[6][:, a * P:(a + 1) * P], xn[:, q, a, :], ident)
                        mm.then_inc(s_xnp, 1)
                    if core:
                        pe.wait_ge(s_kw, n + (B + 1))
                        pe.wait_ge(s_vg, n + (B + 1))
                        chunk_kv(n, p, 0)
                        chunk_out(n, p, 0)
                    if prep:
                        pe.wait_ge(s_mix, n + (B + 2))
                        if not known(n) or n >= 2:
                            pe.wait_ge(s_xa, n + (B - 1))
                        elif n >= 0:
                            pe.wait_ge(s_kw, n + (B + 1))
                        for i, m in enumerate("rk"):
                            mm = pe.matmul(bank[7][:, i * AT:(i + 1) * AT], weight(m), mix[:, i, :],
                                           start=True, stop=True)
                        mm.then_inc(s_rkp, 1)
                    if core:
                        scores(n, p, 1)
                    if prep:
                        pe.wait_ge(s_XT, n + (B + 2))
                        for i, m in ((2, "v"), (3, "g")):
                            for a in range(AG):
                                at = (i - 2) * AT + a * C
                                mm = pe.matmul(bank[6][:, at:at + C], mix[:, i, a * P:(a + 1) * P], weight(m),
                                               start=True, stop=True)
                        mm.then_inc(s_vgp, 1)
                        pe.wait_ge(s_rk, n + (B + 2))
                        for a in range(AG):
                            mm = pe.matmul(bank[7][:, a * C:(a + 1) * C], mix[:, 1, a * P:(a + 1) * P], weight("k"),
                                           start=True, stop=True)
                        mm.then_inc(s_kp, 1)
                    if close:
                        pe.wait_ge(s_z, n + B)
                        if prep:
                            pe.wait_ge(s_vg, n + (B + 2))
                        elif n >= NQ:
                            pe.wait_ge(s_zT, n + (B - 1))
                        for a in range(AG):
                            mm = pe.transpose(bank[6][:, a * P:(a + 1) * P], z[:, a, :], ident)
                        mm.then_inc(s_zp, 1)
                    if core:
                        chunk_kv(n, p, 1)
                        chunk_out(n, p, 1)
                    if close:
                        pe.wait_ge(s_zT, n + B)
                        if prep:
                            pe.wait_ge(s_kw, n + (B + 2))
                        else:
                            pe.wait_ge(s_xa, n + (B - 1))
                        for a in range(AG):
                            mm = pe.matmul(bank[7][:, a * C:(a + 1) * C], zT[:, a * P:(a + 1) * P], weight("o"),
                                           start=True, stop=True)
                        mm.then_inc(s_o, 1)

                steps(pe, -1, 2, 6, NQ, 2, step)

            pe.wait_ge(s_small, 16 * 6)
            front(0)
            front(1)
            experts(0)
            experts(1)
            attention(0)
            front(2)
            attention(1)
            front(3)
            experts(2)
            experts(3)


def _constants():
    import numpy as np
    c = np.zeros((P, NCONST), np.float32)
    p = np.arange(P)

    def put(name, v):
        a, b = CONST[name]
        c[:, a:b] = v
    put("ident", np.eye(P))
    put("before", p[:, None] < p[None, :])
    put("ones", 1.0)
    put("later", p[None, :] > p[:, None])
    put("gap", np.maximum(p[None, :] - p[:, None] - 1, 0))
    put("iota", p[None, :])
    put("block", p[:, None] // HD == p[None, :] // HD)
    put("heads4", (p[:, None] // HD) % HQ == np.arange(HQ)[None, :])
    put("left", (P - 1 - p)[:, None])
    put("rank", (E - np.arange(E))[None, :])
    put("limit", (P * np.arange(T))[None, :])
    put("tile", np.arange(XT + 1)[None, :])
    return c


def kernel(**inputs):
    import numpy as _np
    import concourse.bacc as _bacc
    from concourse import mybir as _mybir
    from concourse.bass_utils import run_bass_kernel_spmd as _run

    def get(name):
        return _np.asarray(inputs["L0_" + name])

    ffn, attn = "ffn_", "attn_"
    decay = _np.repeat(get("attn_time_decay"), HD)
    arrays = {
        "x": get("attn_xq").reshape(HALVES * SEQ, C),
        "consts": _constants(),
        "cols": _np.stack([get("ffn_ln1_g"), get("ffn_ln1_b"), get("ffn_ln2_g"), get("ffn_ln2_b")]
                          + [get("attn_time_mix_" + m).reshape(C) for m in "rkvg"] + [decay], axis=1),
        "rows": _np.stack([_np.broadcast_to(v[None, :], (P, C)) for v in
                           (get("attn_ln_w"), get("attn_ln_b"), decay)], axis=1),
        "bonus": _np.broadcast_to(get("attn_time_faaaa")[None, :], (P, HEADS)),
        "weights": _np.stack([get("ffn_attn_w").T] + [get("attn_W_" + m).T for m in "rkvgo"], axis=1),
        "gate": get("ffn_gate_w").T,
        "wg": get("ffn_gate_proj").transpose(2, 0, 1).reshape(C, E * INTER),
        "wu": get("ffn_up_proj").transpose(2, 0, 1).reshape(C, E * INTER),
        "wd": get("ffn_down_proj").reshape(E, C, CH, P).transpose(3, 0, 2, 1).reshape(P, E * INTER),
    }
    nc = _bacc.Bacc("TRN2", target_bir_lowering=False, num_devices=1)
    launch, args = {}, []
    for name, a in arrays.items():
        a = _np.ascontiguousarray(a)
        launch[f"in_{name}"] = a
        args.append(nc.dram_tensor(f"in_{name}", a.shape, _mybir.dt.from_np(a.dtype), kind="ExternalInput").ap())
    out = nc.dram_tensor("out_x", (HALVES * SEQ, C), F32, kind="ExternalOutput").ap()
    macaron(nc, *args, out)
    r = _run(nc, [launch], core_ids=[0])
    return r.results[0]["out_x"].reshape(HALVES, SEQ, C)
```

```python
from contextlib import ExitStack

import concourse.bass as bass
from concourse import mybir

F32 = mybir.dt.float32
I32 = mybir.dt.int32
ALU = mybir.AluOpType
ACT = mybir.ActivationFunctionType
AX = mybir.AxisListType.X

P = 128
C = 128
HALVES = 2
SEQ = 2048
T = SEQ // P
GROUP = 4
G = T // GROUP
E = 8
INTER = 512
CH = INTER // P
TOP = 2
HEADS = 16
HD = C // HEADS
HQ = 32 // HD
EPS = 1e-5
XT = (SEQ * TOP + E * (P - 1)) // P
SLOTS = XT * P
FILL = 3
BIG = 3.0e38
DECAY_MAX = 1.0e30
AG = 2
AT = AG * P
NQ = T // AG
QUADS = C // 32
VQ = HQ * (32 + HD)

CONST = {}
_at = 0
for _name, _width in (("ident", P), ("before", P), ("ones", P), ("later", P), ("gap", P), ("iota", P),
                      ("block", P), ("centre", P), ("average", P), ("eps", 1), ("heads4", HQ), ("left", 1), ("rank", E), ("limit", T), ("tile", XT + 1)):
    CONST[_name] = (_at, _at + _width)
    _at += _width
NCONST = _at
COLS = ("ln1_g", "ln1_b", "ln2_g", "ln2_b", "mix_r", "mix_k", "mix_v", "mix_g", "decay", "ln_w", "ln_b")
ROWS = ("decay",)
WEIGHTS = ("proj", "r", "k", "v", "g", "o")

ORD = ("A1", "B1", "A2", "B2")


class Chain:

    def __init__(self, eng, sem, base=0):
        self.eng, self.sem, self.base, self.n = eng, sem, base, 0

    def step(self, ins):
        ins.then_inc(self.sem, 1)
        self.n += 1

    def wait(self):
        self.eng.wait_ge(self.sem, self.base + self.n)


def steps(eng, first, lo, hi, last, unroll, step):
    assert (hi - lo) % unroll == 0
    for n in range(first, lo):
        step(n, n % unroll)
    with eng.Fori(0, (hi - lo) // unroll) as i:
        for k in range(unroll):
            step(i * unroll + (lo + k), (lo + k) % unroll)
    for n in range(hi, last + 1):
        step(n, n % unroll)


def attention_steps(eng, last, inside, step):
    if not inside:
        return steps(eng, -1, 2, 6, last, 2, step)
    for n in range(-1, max(*inside) + 2):
        step(n, n % 2)


def group_no(group):
    return group[0] * G + group[1]


def known(n):
    return isinstance(n, int)


def macaron(nc, x_in, consts_in, cols_in, rows_in, bonus_in, weights_in, gate_in, wg_in, wu_in, wd_in, out):
    with ExitStack() as ctx:
        def sb(name, shape, dt=F32):
            return ctx.enter_context(nc.sbuf_tensor(name, shape, dt))

        def sem(name):
            return ctx.enter_context(nc.semaphore(name))

        bank = [ctx.enter_context(nc.psum_tensor(f"bank{i}", [P, 512], F32)) for i in range(8)]

        X = sb("X", [P, HALVES * T, C])
        H = sb("H", [P, HALVES * T, C])
        consts = sb("consts", [P, NCONST])
        cols = sb("cols", [P, len(COLS)])
        rows = sb("rows", [P, len(ROWS), C])
        bonus = sb("bonus", [P, HEADS])
        weights = sb("weights", [P, len(WEIGHTS), C])
        gate = sb("gate", [P, E])
        wg = sb("wg", [P, E * INTER])
        wu = sb("wu", [P, E * INTER])
        wd = sb("wd", [P, E * INTER])

        def const(name):
            a, b = CONST[name]
            return consts[:, a:b]

        def col(name):
            i = COLS.index(name)
            return cols[:, i:i + 1]

        def row(name):
            return rows[:, ROWS.index(name), :]

        def weight(name):
            return weights[:, WEIGHTS.index(name), :]

        ident = const("ident")

        mv = sb("mv", [P, 2, GROUP, 2])
        bn = sb("bn", [P, GROUP, 6])
        var2 = sb("var2", [P, 2, 2, GROUP])
        root = sb("root", [P, 2, 2, GROUP])
        rstd = sb("rstd", [P, 2, 2, GROUP])
        mv2 = sb("mv2", [P, 2, GROUP, 2])
        root2 = sb("root2", [P, 2, GROUP])
        rstd2 = sb("rstd2", [P, 2, GROUP])
        n1 = sb("n1", [P, 2, GROUP, C])
        n2T = sb("n2T", [P, 2, GROUP * P])
        L = sb("L", [P, T, E])
        L2 = sb("L2", [P, T, E])
        eq = sb("eq", [P, T, E])
        pick = sb("pick", [P, TOP, T, E])
        both = sb("both", [P, T, E])
        best = sb("best", [P, TOP, T])
        first = sb("first", [P, T])
        gap2 = sb("gap2", [P, T])
        wexp = sb("wexp", [P, T])
        wden = sb("wden", [P, T])
        share = sb("share", [P, HALVES, TOP, T])
        counts = sb("counts", [P, E, T])
        ahead = sb("ahead", [P, T, E])
        cum = sb("cum", [P, E, T])
        ones_et = sb("ones_et", [P, E, T])
        over = sb("over", [P, E, T])
        tiles_e = sb("tiles_e", [P, E])
        ends = sb("ends", [P, E])
        start = sb("start", [P, E])
        slot_e = sb("slot_e", [P, T, E])
        slot_f = sb("slot_f", [P, TOP, T])
        slot = sb("slot", [P, HALVES, TOP, T], I32)
        done_e = sb("done_e", [P, XT + 1, E])
        tile_ef = sb("tile_ef", [P, XT + 1])
        tile_e = sb("tile_e", [P, HALVES, XT + 1], I32)
        slots_io = sb("slots_io", [P, 8 * C])
        xs = slots_io[:, 0:4 * C].rearrange("p (k c) -> p k c", k=4)
        ys = slots_io[:, 4 * C:8 * C].rearrange("p (k c) -> p k c", k=4)
        mix = slots_io[:].rearrange("p (m i) -> p m i", m=4)
        xsT = sb("xsT", [P, 2, P])
        shared = sb("shared", [P, 2 * HEADS * P])
        sg, hid, hidT, n1T = (shared[:, i * 2 * INTER:(i + 1) * 2 * INTER].rearrange("p (b i) -> p b i", b=2)
                         for i in range(4))
        att = shared[:].rearrange("p (b h i) -> p b h i", b=2, h=HEADS)
        Y = sb("Y", [P, TOP, T, C])
        n2a = sb("n2a", [P, T, C])
        n2 = (n2a[:], Y[:, 1])
        zero = Y[:, 0, 0:SLOTS // FILL // P, :]

        wm = sb("wm", [P, HEADS, P])
        negd_col = sb("negd_col", [P, 1])
        expd_col = sb("expd_col", [P, 1])
        expd_row = sb("expd_row", [P, C])
        negd_row = sb("negd_row", [P, C])
        w_chunk = sb("w_chunk", [P, 1])
        w_since = sb("w_since", [P, P])
        w_until = sb("w_until", [P, C])
        amv = sb("amv", [P, HALVES, T, 2])
        abn = sb("abn", [P, T, 6])
        aroot = sb("aroot", [P, HALVES, T])
        arstd = sb("arstd", [P, HALVES, T])
        xn = sb("xn", [P, AG, C])
        xT = sb("xT", [P, 2, AT + 1])
        delta = sb("delta", [P, AT])
        rT = sb("rT", [P, AG, P])
        kz = sb("kz", [P, 2, 4, AT])
        rx = sb("rx", [P, 2, AG, HQ, P])
        rw = sb("rw", [P, 2, AG, P])
        kw = sb("kw", [P, 2, AG, C])
        vz = sb("vz", [P, 2, AG, QUADS, VQ])
        gT = sb("gT", [P, 2, AT])
        state = sb("state", [P, 2, C])
        add = sb("add", [P, C])
        yT = sb("yT", [P, AT])
        yc = sb("yc", [P, AT])
        sq = sb("sq", [P, AT])
        yn = sq
        yroot = sb("yroot", [P, AT])
        zT = sb("zT", [P, AT])

        slot_rows = [nc.dram_tensor(f"slot_rows{h}", (SLOTS, C), F32, kind="Internal").ap() for h in range(HALVES)]
        y_rows = [nc.dram_tensor(f"y_rows{h}", (SLOTS, C), F32, kind="Internal").ap() for h in range(HALVES)]

        s_x = [sem(f"x_loaded{g}") for g in range(HALVES * G)]
        s_small = sem("small_loaded")
        s_big = sem("expert_weights_loaded")
        s_zero = sem("zero_ready")
        s_filled = sem("slots_filled")
        s_dve = sem("vector_step")
        s_var = sem("variances")
        s_root = sem("roots")
        s_n1 = sem("n1_ready")
        s_n1p = sem("n1_transposed")
        s_n1T = sem("n1T_ready")
        s_proj = sem("proj_done")
        s_var2 = sem("variances2")
        s_root2 = sem("roots2")
        s_n2 = sem("n2_ready")
        s_n2p = sem("n2_transposed")
        s_n2T = sem("n2T_ready")
        s_logit = sem("logits_done")
        s_h = sem("h_ready")
        s_cntc = sem("counts_copied")
        s_logc = sem("logits_copied")
        s_gap = sem("top_gap_ready")
        s_exp = sem("top_exp_ready")
        s_pick = sem("picks_ready")
        s_count = sem("counts_done")
        s_table = sem("slots_ready")
        s_scat = [sem(f"rows_scattered{h}") for h in range(HALVES)]
        s_load = [sem(f"slot_rows_loaded{k}") for k in range(4)]
        s_xp = sem("xs_transposed")
        s_xT = sem("xsT_ready")
        s_gu = sem("gate_up_done")
        s_sg = sem("silu_ready")
        s_hid = sem("hidden_ready")
        s_hp = sem("hidden_transposed")
        s_hT = sem("hiddenT_ready")
        s_y = sem("down_done")
        s_yc = sem("y_copied")
        s_store = [sem(f"y_stored{k}") for k in range(4)]
        s_got = [sem(f"y_gathered{g}") for g in range(G)]
        s_comb = sem("combined")
        s_out = sem("output_stored")

        s_tab = sem("decay_tables_step")
        s_tabv = sem("decay_tables_ready")
        s_avar = sem("attn_variances")
        s_aroot = sem("attn_roots")
        s_xn = sem("xn_ready")
        s_xnp = sem("xn_transposed")
        s_XT = sem("XT_ready")
        s_delta = sem("delta_ready")
        s_mix = sem("mix_ready")
        s_rkp = sem("rk_projected")
        s_kz = sem("k_zeroed")
        s_rk = sem("rk_ready")
        s_vgp = sem("vg_projected")
        s_vg = sem("vg_ready")
        s_kp = sem("k_rows_projected")
        s_kw = sem("kw_ready")
        s_rx = sem("rx_ready")
        s_sc = sem("scores_done")
        s_att = sem("att_ready")
        s_kv = sem("kv_done")
        s_add = sem("kv_masked")
        s_state = sem("state_ready")
        s_av = sem("chunk_output_done")
        s_y8 = sem("chunk_outputs_copied")
        s_vz = sem("v_padding_zeroed")
        s_cen = sem("centred")
        s_sq = sem("squared")
        s_yvar = sem("head_variances")
        s_yroot = sem("head_roots")
        s_yrstd = sem("head_rstd_ready")
        s_yn = sem("normalized")
        s_z = sem("z_ready")
        s_o = sem("attn_out_done")
        s_xa = sem("attn_added")

        block = ctx.enter_context(nc.Block())
        RUNS = [(0, 0), (0, 1), (1, 0), (1, 1)]
        NXT = XT

        INSIDE = {0: (2, 0), 1: (2, 1), 2: (2, 2), 3: (2, 3), 5: (3, 0), 6: (3, 1), 8: (3, 2), NQ + 2: (3, 3)}
        ROUTE = {4: 2, NQ + 3: 3}

        LO, HI, UN = 3, 35, 4

        def v_own(q, a):
            return vz[:, q, a].rearrange("p q (l x) -> p q l x", l=HQ)[:, :, :, 0:HD]

        @block.sync
        def _(sp):
            sp.dma_start(consts[:], consts_in).then_inc(s_small, 16)
            sp.dma_start(cols[:], cols_in).then_inc(s_small, 16)
            sp.dma_start(weights[:], weights_in).then_inc(s_small, 16)
            sp.dma_start(gate[:], gate_in).then_inc(s_small, 16)
            sp.dma_start(rows[:], rows_in).then_inc(s_small, 16)
            sp.dma_start(bonus[:], bonus_in).then_inc(s_small, 16)
            for g in range(HALVES * G):
                sp.dma_start(X[:, g * GROUP:(g + 1) * GROUP, :],
                             x_in[g * GROUP * P:(g + 1) * GROUP * P, :].rearrange("(t p) c -> p t c", p=P)
                             ).then_inc(s_x[g], 16)
            sp.wait_ge(s_zero, 1)
            for h in range(HALVES):
                for q in range(FILL):
                    n = SLOTS // FILL
                    sp.dma_start(slot_rows[h][q * n:(q + 1) * n, :].rearrange("(p a) c -> p a c", p=P),
                                 zero).then_inc(s_filled, 16)
            for dst, src in ((wg, wg_in), (wu, wu_in), (wd, wd_in)):
                sp.dma_start(dst[:], src).then_inc(s_big, 16)

            for run, (layer, half) in enumerate(RUNS):
                base = run * NXT
                sp.wait_ge(s_scat[half], 16 * TOP * T * (layer + 1))
                if run == 2:
                    sp.wait_ge(s_kp, 2 * NQ)

                def load(n, k):
                    if not known(n) or base + n >= 4:
                        sp.wait_ge(s_xp, n + (base - 3))
                    sp.dma_start(xs[:, k, :], slot_rows[half][bass.ds(n * P, P), :]).then_inc(s_load[k], 16)

                def store(n, k):
                    sp.wait_ge(s_yc, n + (base + 1))
                    sp.dma_start(y_rows[half][bass.ds(n * P, P), :], ys[:, k, :]).then_inc(s_store[k], 16)

                def step(n, k):
                    if not known(n) or n < NXT:
                        load(n, (base + k) % 4)
                    if not known(n) or n >= 5:
                        store(n - 5, (base + k - 5) % 4)

                steps(sp, 0, 5, 37, NXT + 4, 4, step)
            for half in range(HALVES):
                for g in range(G):
                    sp.wait_ge(s_comb, (2 + half) * G + g + 1)
                    t = half * T + g * GROUP
                    sp.dma_start(out[t * P:(t + GROUP) * P, :].rearrange("(t p) c -> p t c", p=P),
                                 X[:, t:t + GROUP, :]).then_inc(s_out, 16)
            sp.wait_ge(s_out, 16 * HALVES * G)

        @block.gpsimd
        def _(pool):
            pool.memset(zero, 0.0).then_inc(s_zero, 1)
            pool.memset(vz[:], 0.0).then_inc(s_vz, 1)

            def scatter(run):
                layer, half = RUNS[run]
                if layer == 0:
                    pool.wait_ge(s_filled, 16 * FILL * HALVES)
                pool.wait_ge(s_table, run + 1)
                for t in range(T):
                    for k in range(TOP):
                        pool.indirect_dma_start(
                            slot_rows[half], bass.IndirectOffsetOnAxis(slot[:, half, k, t:t + 1], 0),
                            n2[half][:, t, :], None).then_inc(s_scat[half], 16)

            def gather(run):
                layer, half = RUNS[run]
                for k in range(4):
                    pool.wait_ge(s_store[k], 16 * len([n for n in range((run + 1) * NXT) if n % 4 == k]))
                if run:
                    pool.wait_ge(s_comb, run * G)
                for t in range(T):
                    for k in range(TOP):
                        pool.indirect_dma_start(
                            Y[:, k, t, :], None, y_rows[half],
                            bass.IndirectOffsetOnAxis(slot[:, half, k, t:t + 1], 0)
                        ).then_inc(s_got[t // GROUP], 16)

            scatter(0)
            scatter(1)
            gather(0)
            gather(1)
            scatter(2)
            scatter(3)
            gather(2)
            gather(3)

        @block.scalar
        def _(act):
            def fronts():
                for s in range(HALVES * G + 4):
                    if s < HALVES * G:
                        roots(s)
                    if 0 <= s - 1 < HALVES * G:
                        n1_out(s - 1, bank[(s - 1) % 2])
                    if 0 <= s - 2 < HALVES * G:
                        roots2(s - 2)
                    if 0 <= s - 3 < HALVES * G:
                        n2_out(s - 3, bank[4 + (s - 3) % 2])
                    if s - 3 in (G, 2 * G):
                        top_exp((s - 3) // G - 1)

            def roots(m):
                act.wait_ge(s_var, m + 1)
                act.activation(root[:, m % 2], var2[:, m % 2], ACT.Sqrt).then_inc(s_root, 1)

            def n1_out(m, src):
                act.wait_ge(s_n1p, m + 1)
                act.activation(n1T[:, m % 2, :], src[:], ACT.Identity,
                               bias=col("ln1_b"), scale=col("ln1_g")).then_inc(s_n1T, 1)

            def roots2(m):
                act.wait_ge(s_var2, m + 1)
                act.activation(root2[:, m % 2], mv2[:, m % 2, :, 1], ACT.Sqrt).then_inc(s_root2, 1)

            def n2_out(m, src):
                act.wait_ge(s_n2p, m + 1)
                act.activation(n2T[:, m % 2, :], src[:], ACT.Identity,
                               bias=col("ln2_b"), scale=col("ln2_g")).then_inc(s_n2T, 1)

            def top_exp(run):
                act.wait_ge(s_gap, run + 1)
                act.activation(wexp[:], gap2[:], ACT.Exp).then_inc(s_exp, 1)

            def experts(run):
                base = run * NXT

                def step(n, k):
                    k2 = (base + k) % 2
                    if not known(n) or n + 1 < NXT:
                        act.wait_ge(s_xp, n + (base + 2))
                        act.activation(xsT[:, 1 - k2, :], bank[0][:, 0:P], ACT.Identity,
                                       bias=col("ln2_b"), scale=col("ln2_g")).then_inc(s_xT, 1)
                    if not known(n) or 0 <= n < NXT:
                        act.wait_ge(s_gu, n + (base + 1))
                        act.activation(sg[:, k2, :], bank[1 + k2][:], ACT.Silu).then_inc(s_sg, 1)
                    if not known(n) or 1 <= n < NXT + 1:
                        act.wait_ge(s_hp, n + base)
                        act.activation(hidT[:, 1 - k2, :], bank[5 + (1 - k2)][:], ACT.Copy).then_inc(s_hT, 1)

                steps(act, -1, LO, HI, NXT, UN, step)

            def tables():
                act.activation(expd_col[:], col("decay"), ACT.Exp)
                act.activation(expd_row[:], row("decay"), ACT.Exp).then_inc(s_tab, 1)
                act.wait_ge(s_tabv, 1)
                act.activation(w_chunk[:], negd_col[:], ACT.Exp, scale=float(P))
                act.activation(w_since[:], const("iota"), ACT.Exp, scale=negd_col[:])
                act.activation(w_until[:], negd_row[:], ACT.Exp, scale=const("left"))
                for h in range(HEADS):
                    ins = act.activation(wm[:, h, :], const("gap"), ACT.Exp, scale=negd_row[:, h * HD:h * HD + 1])
                ins.then_inc(s_tab, 1)

            def attention(half, inside={}, route={}):
                B = half * NQ
                act.wait_ge(s_kz, 1)
                act.wait_ge(s_vz, 1)
                act.wait_ge(s_avar, half + 1)
                act.activation(aroot[:, half], amv[:, half, :, 1], ACT.Sqrt).then_inc(s_aroot, 1)

                def step(n, p):
                    q = 1 - p
                    prep = not known(n) or n + 1 < NQ
                    close = not known(n) or 1 <= n <= NQ
                    if close:
                        act.wait_ge(s_cen, n + B)
                        if not known(n) or n + B >= 2:
                            act.wait_ge(s_z, n + (B - 1))
                        act.activation(yc[:], bank[4][:, AT:2 * AT], ACT.Copy)
                        act.activation(sq[:], bank[4][:, AT:2 * AT], ACT.Square).then_inc(s_sq, 1)
                        act.wait_ge(s_yvar, n + B)
                        act.activation(yroot[:], bank[4][:, 0:AT], ACT.Sqrt, bias=const("eps")).then_inc(s_yroot, 1)
                    if prep:
                        act.wait_ge(s_xnp, n + (B + 2))
                        if known(n) and n == -1:
                            act.activation(xT[:, q, 0:1], consts[:, 0:1], ACT.Copy, scale=0.0)
                        else:
                            act.wait_ge(s_XT, n + (B + 1))
                            act.activation(xT[:, q, 0:1], xT[:, p, AT:AT + 1], ACT.Copy)
                        act.activation(xT[:, q, 1:AT + 1], bank[6][:, 0:AT], ACT.Copy).then_inc(s_XT, 1)
                    if known(n) and n in inside:
                        n1_out(group_no(inside[n]), bank[5])
                        roots2(group_no(inside[n]))
                    if known(n) and n in route:
                        top_exp(route[n])
                    if prep:
                        act.wait_ge(s_rkp, n + (B + 2))
                        if not known(n) or n + B >= 0:
                            act.wait_ge(s_rx, n + (B + 1))
                        act.activation(rT[:], bank[7][:, 0:AT].rearrange("p (a t) -> p a t", a=AG), ACT.Copy)
                        for i in range(QUADS):
                            own = slice(32 * i, 32 * i + 32)
                            ins = act.activation(kz[own, q, i, :], bank[7][own, AT:2 * AT], ACT.Copy)
                        ins.then_inc(s_rk, 1)
                        act.wait_ge(s_vgp, n + (B + 2))
                        if close:
                            act.wait_ge(s_z, n + B)
                        for a in range(AG):
                            act.activation(v_own(q, a),
                                           bank[6][:, a * C:(a + 1) * C].rearrange("p (q l d) -> p q l d", l=HQ, d=HD),
                                           ACT.Copy)
                        act.activation(gT[:, q], bank[6][:, AT:2 * AT], ACT.Silu).then_inc(s_vg, 1)
                    if known(n) and n in inside:
                        n2_out(group_no(inside[n]), bank[5])
                    if not known(n) or 0 <= n < NQ:
                        act.wait_ge(s_av, n * 2 + (2 * B + 2))
                        act.activation(yT[:], bank[4][:, 0:AT], ACT.Copy, scale=1.0 / HD).then_inc(s_y8, 1)
                    if known(n) and n + 1 in inside:
                        roots(group_no(inside[n + 1]))

                attention_steps(act, NQ, inside, step)

            act.wait_ge(s_small, 16 * 6)
            fronts()
            tables()
            experts(0)
            experts(1)
            attention(0)
            attention(1, INSIDE, ROUTE)
            experts(2)
            experts(3)

        def stored(n, k, base):
            rest = (base + k - 2) % 4
            if known(n):
                return 16 * ((base + n - 2) // 4)
            return n * 4 + (4 * (base - 2 - rest))

        @block.vector
        def _(dve):
            link = Chain(dve, s_dve)

            def norm_stats(run, s):
                n = run * G + s
                par = n % 2
                t0 = RUNS[run][1] * T + s * GROUP
                if run == 0 or run == 1:
                    dve.wait_ge(s_x[run * G + s], 16)
                link.wait()
                for t in range(GROUP):
                    link.step(dve.bn_stats(bn[:, t, :], X[:, t0 + t, :]))
                link.wait()
                for t in range(GROUP):
                    link.step(dve.bn_aggr(mv[:, par, t, :], bn[:, t, :]))
                link.wait()
                link.step(dve.tensor_scalar(var2[:, par, 0, :], mv[:, par, :, 1], EPS, None, ALU.add))
                dve.tensor_scalar(var2[:, par, 1, :], mv[:, par, :, 1], 1.0 + EPS, EPS * EPS,
                                  ALU.mult, ALU.add).then_inc(s_var, 1)
                link.wait()

            def norm_apply(run, s):
                n = run * G + s
                par = n % 2
                t0 = RUNS[run][1] * T + s * GROUP
                dve.wait_ge(s_root, n + 1)
                link.step(dve.reciprocal(rstd[:, par], root[:, par]))
                link.wait()
                if n >= 2:
                    dve.wait_ge(s_n1p, n - 1)
                for t in range(GROUP):
                    ins = dve.tensor_scalar(n1[:, par, t, :], X[:, t0 + t, :], mv[:, par, t, 0:1],
                                            rstd[:, par, 1, t:t + 1], ALU.subtract, ALU.mult)
                ins.then_inc(s_n1, 1)
                for t in range(GROUP):
                    link.step(dve.tensor_scalar(H[:, t0 + t, :], X[:, t0 + t, :], mv[:, par, t, 0:1],
                                                rstd[:, par, 0, t:t + 1], ALU.subtract, ALU.mult))

            def add_proj(run, s, src=None):
                n = run * G + s
                par = n % 2
                t0 = RUNS[run][1] * T + s * GROUP
                dve.wait_ge(s_proj, n + 1)
                link.wait()
                hg = H[:, t0:t0 + GROUP, :]
                src = src or bank[2 + par]
                dve.tensor_tensor(hg, hg, src[:].rearrange("p (t c) -> p t c", c=C), ALU.add).then_inc(s_h, 1)
                dve.wait_ge(s_h, n + 1)
                for t in range(GROUP):
                    link.step(dve.bn_stats(bn[:, t, :], H[:, t0 + t, :]))
                link.wait()
                for t in range(GROUP):
                    link.step(dve.bn_aggr(mv2[:, par, t, :], bn[:, t, :]))
                link.wait()
                dve.tensor_scalar(mv2[:, par, :, 1], mv2[:, par, :, 1], EPS, None, ALU.add).then_inc(s_var2, 1)

            def norm2_apply(run, s):
                n = run * G + s
                par = n % 2
                layer, half = RUNS[run]
                t0 = half * T + s * GROUP
                dve.wait_ge(s_root2, n + 1)
                link.step(dve.reciprocal(rstd2[:, par], root2[:, par]))
                link.wait()
                if layer and s == 0:
                    dve.wait_ge(s_scat[half], 16 * TOP * T * layer)
                for t in range(GROUP):
                    ins = dve.tensor_scalar(n2[half][:, s * GROUP + t, :], H[:, t0 + t, :], mv2[:, par, t, 0:1],
                                            rstd2[:, par, t:t + 1], ALU.subtract, ALU.mult)
                ins.then_inc(s_n2, 1)

            def logits(run, s, src=bank[6]):
                n = run * G + s
                dve.wait_ge(s_logit, n + 1)
                dve.tensor_copy(L[:, s * GROUP:(s + 1) * GROUP, :],
                                src[:, 0:GROUP * E].rearrange("p (t e) -> p t e", e=E)).then_inc(s_logc, 1)

            def per_tile(v):
                return v.unsqueeze(2).broadcast_to([P, T, E])

            def per_expert(v, n=T):
                return v.unsqueeze(1).broadcast_to([P, n, E])

            def route(run):
                route_picks(run)
                route_counts(run, bank[7])
                route_slots(run)

            def route_picks(run):
                layer, half = RUNS[run]
                rank = per_expert(const("rank"))
                dve.wait_ge(s_logc, (run + 1) * G)
                src = L
                for k in range(TOP):
                    link.step(dve.tensor_reduce(best[:, k], src[:], AX, ALU.max))
                    link.wait()
                    link.step(dve.tensor_tensor(eq[:], src[:], per_tile(best[:, k]), ALU.is_equal))
                    link.wait()
                    link.step(dve.tensor_tensor(eq[:], eq[:], rank, ALU.mult))
                    link.wait()
                    link.step(dve.tensor_reduce(first[:], eq[:], AX, ALU.max))
                    link.wait()
                    link.step(dve.tensor_tensor(pick[:, k], rank, per_tile(first[:]), ALU.is_equal))
                    link.wait()
                    if k == 0:
                        link.step(dve.scalar_tensor_tensor(L2[:], pick[:, 0], -BIG, L[:], ALU.mult, ALU.add))
                        link.wait()
                        src = L2
                dve.tensor_tensor(gap2[:], best[:, 1], best[:, 0], ALU.subtract).then_inc(s_gap, 1)
                dve.tensor_tensor(both[:], pick[:, 0], pick[:, 1], ALU.add).then_inc(s_pick, 1)

            def route_counts(run, src):
                dve.wait_ge(s_count, run + 1)
                link.wait()
                dve.tensor_copy(counts[:], src[:, T * E:2 * T * E].rearrange("p (t e) -> p e t", e=E))
                dve.tensor_copy(ahead[:], src[:, 0:T * E].rearrange("p (t e) -> p t e", e=E)).then_inc(s_cntc, 1)

            def route_slots(run):
                layer, half = RUNS[run]
                dve.wait_ge(s_exp, run + 1)
                link.step(dve.tensor_scalar(wden[:], wexp[:], 1.0, 2.0, ALU.add, ALU.mult))
                link.wait()
                link.step(dve.reciprocal(share[:, half, 0], wden[:]))
                link.wait()
                link.step(dve.tensor_tensor(share[:, half, 1], share[:, half, 0], wexp[:], ALU.mult))
                dve.wait_ge(s_cntc, run + 1)
                ones = ones_et[:].rearrange("p e t -> p (e t)")
                link.step(dve.tensor_tensor_scan(cum[:].rearrange("p e t -> p (e t)"), ones,
                                                 counts[:].rearrange("p e t -> p (e t)"), 0.0, ALU.mult, ALU.add))
                link.wait()
                link.step(dve.tensor_tensor(over[:], cum[:, :, T - 1:T].broadcast_to([P, E, T]),
                                            const("limit").unsqueeze(1).broadcast_to([P, E, T]), ALU.is_gt))
                link.wait()
                link.step(dve.tensor_reduce(tiles_e[:], over[:], AX, ALU.add))
                link.wait()
                link.step(dve.tensor_tensor_scan(ends[:], const("ones")[:, 0:E], tiles_e[:], 0.0, ALU.mult, ALU.add))
                link.wait()
                link.step(dve.tensor_tensor(start[:], ends[:], tiles_e[:], ALU.subtract))
                link.wait()
                link.step(dve.tensor_tensor(cum[:], cum[:], counts[:], ALU.subtract))
                link.wait()
                link.step(dve.tensor_tensor(slot_e[:], cum[:].rearrange("p e t -> p t e"), ahead[:], ALU.add))
                link.wait()
                link.step(dve.scalar_tensor_tensor(slot_e[:], per_expert(start[:]), float(P), slot_e[:],
                                                   ALU.mult, ALU.add))
                for k in range(TOP):
                    link.wait()
                    link.step(dve.tensor_tensor(eq[:], slot_e[:], pick[:, k], ALU.mult))
                    link.wait()
                    link.step(dve.tensor_reduce(slot_f[:, k], eq[:], AX, ALU.add))
                n = XT + 1
                link.step(dve.tensor_tensor(done_e[:], per_expert(ends[:], n),
                                            const("tile").unsqueeze(2).broadcast_to([P, n, E]), ALU.is_le))
                link.wait()
                link.step(dve.tensor_reduce(tile_ef[:], done_e[:], AX, ALU.add))
                link.wait()
                link.step(dve.tensor_scalar(tile_e[:, half], tile_ef[:], float(E - 1), float(INTER),
                                            ALU.min, ALU.mult))
                link.wait()
                dve.tensor_copy(slot[:, half], slot_f[:]).then_inc(s_table, 1)

            def fronts():
                for s in range(HALVES * G + 4):
                    if s < HALVES * G:
                        norm_stats(s // G, s % G)
                    if 0 <= s - 1 < HALVES * G:
                        norm_apply((s - 1) // G, (s - 1) % G)
                    if 0 <= s - 2 < HALVES * G:
                        add_proj((s - 2) // G, (s - 2) % G)
                    if 0 <= s - 3 < HALVES * G:
                        norm2_apply((s - 3) // G, (s - 3) % G)
                    if 0 <= s - 4 < HALVES * G:
                        logits((s - 4) // G, (s - 4) % G)
                    if s - 3 in (G, 2 * G):
                        route((s - 3) // G - 1)

            def experts(run, after=None):
                base = run * NXT

                def step(n, k):
                    k2 = (base + k) % 2
                    if not known(n) or n < NXT:
                        dve.wait_ge(s_sg, n + (base + 1))
                        dve.tensor_tensor(hid[:, k2, :], sg[:, k2, :], bank[3 + k2][:],
                                          ALU.mult).then_inc(s_hid, 1)
                    if not known(n) or n >= 2:
                        j = (base + k - 2) % 4
                        dve.wait_ge(s_y, n + (base - 1))
                        if not known(n) or base + n - 2 >= 4:
                            dve.wait_ge(s_store[j], stored(n, k, base))
                        dve.tensor_copy(ys[:, j, :], bank[7][:, 0:C]).then_inc(s_yc, 1)

                    if after and known(n) and HI <= n < HI + G:
                        after(n - HI)

                steps(dve, 0, LO, HI, NXT + 1, UN, step)

            def combine(run, g):
                layer, half = RUNS[run]
                t0 = half * T + g * GROUP
                dve.wait_ge(s_got[g], 16 * GROUP * TOP * (run + 1))
                xg = X[:, t0:t0 + GROUP, :]
                link.wait()
                link.step(dve.scalar_tensor_tensor(xg, H[:, t0:t0 + GROUP, :], 0.5, xg, ALU.mult, ALU.add))
                link.wait()
                for k in range(TOP):
                    for t in range(GROUP):
                        ins = dve.scalar_tensor_tensor(
                            X[:, t0 + t, :], Y[:, k, g * GROUP + t, :], share[:, half, k, g * GROUP + t:g * GROUP + t + 1],
                            X[:, t0 + t, :], ALU.mult, ALU.add)
                        if k == 0:
                            link.step(ins)
                    if k == 0:
                        link.wait()
                ins.then_inc(s_comb, 1)

            def combine_stats(run, g):
                half = RUNS[run][1]
                combine(run, g)
                dve.wait_ge(s_comb, run * G + g + 1)
                link.wait()
                for t in range(g * GROUP, (g + 1) * GROUP):
                    link.step(dve.bn_stats(abn[:, t, :], X[:, half * T + t, :]))
                link.wait()
                for t in range(g * GROUP, (g + 1) * GROUP):
                    link.step(dve.bn_aggr(amv[:, half, t, :], abn[:, t, :]))

            def tables():
                dve.wait_ge(s_tab, 1)
                dve.tensor_scalar(negd_col[:], expd_col[:], DECAY_MAX, -1.0, ALU.min, ALU.mult)
                dve.tensor_scalar(negd_row[:], expd_row[:], DECAY_MAX, -1.0, ALU.min, ALU.mult).then_inc(s_tabv, 1)
                dve.wait_ge(s_tab, 2)
                link.step(dve.tensor_tensor(wm[:], wm[:], const("later").unsqueeze(1).broadcast_to([P, HEADS, P]),
                                            ALU.mult))
                link.wait()
                for h in range(HEADS):
                    link.step(dve.scalar_tensor_tensor(wm[:, h, :], ident, bonus[:, h:h + 1], wm[:, h, :],
                                                       ALU.mult, ALU.add))

            def attn_roots(half):
                link.wait()
                dve.tensor_scalar(amv[:, half, :, 1], amv[:, half, :, 1], EPS, None, ALU.add).then_inc(s_avar, 1)
                link.step(dve.memset(state[:, 0, :], 0.0))
                dve.wait_ge(s_aroot, half + 1)
                link.step(dve.reciprocal(arstd[:, half], aroot[:, half]))
                link.wait()

            def attention(half, inside={}, route={}):
                B = half * NQ
                attn_roots(half)
                if half == 0:
                    for k in range(4):
                        dve.wait_ge(s_store[k], 16 * len([n for n in range(2 * NXT) if n % 4 == k]))

                def mask(n, c):
                    if not known(n) or n >= 1:
                        dve.wait_ge(s_av, n * 2 + (2 * B - 1 + c))
                    for q in range(4):
                        dve.wait_ge(s_sc, n * 8 + (8 * B + 4 * c + q + 1))
                        dve.tensor_tensor(att[:, c, 4 * q:4 * q + 4, :],
                                          bank[q][:].rearrange("p (h i) -> p h i", i=P),
                                          wm[:, 4 * q:4 * q + 4, :], ALU.mult).then_inc(s_att, 1)

                def group_norm(n, q):
                    dve.wait_ge(s_yroot, n + B)
                    dve.reciprocal(yroot[:], yroot[:]).then_inc(s_yrstd, 1)
                    dve.wait_ge(s_yrstd, n + B)
                    dve.scalar_tensor_tensor(yn[:], yc[:], col("ln_w"), yroot[:], ALU.mult, ALU.mult).then_inc(s_yn, 1)
                    dve.wait_ge(s_yn, n + B)
                    dve.wait_ge(s_vg, n + B)
                    if not known(n) or n + B >= 2:
                        dve.wait_ge(s_o, n + (B - 1))
                    dve.scalar_tensor_tensor(zT[:], yn[:], col("ln_b"), gT[:, q], ALU.add, ALU.mult).then_inc(s_z, 1)

                def update(n, c):
                    dve.wait_ge(s_kv, n * 2 + (2 * B + c + 1))
                    if c == 1 or not known(n) or n >= 1:
                        dve.wait_ge(s_state, n * 2 + (2 * B + c))
                    dve.tensor_tensor(add[:], bank[5][:, 0:C], const("block"), ALU.mult).then_inc(s_add, 1)
                    dve.wait_ge(s_add, n * 2 + (2 * B + c + 1))
                    if c == 1 or not known(n) or n >= 1:
                        dve.wait_ge(s_av, n * 2 + (2 * B + c))
                    dve.scalar_tensor_tensor(state[:, 1 - c, :], state[:, c, :], w_chunk[:], add[:],
                                             ALU.mult, ALU.add).then_inc(s_state, 1)

                def step(n, p):
                    prep = not known(n) or n + 1 < NQ
                    core = not known(n) or 0 <= n < NQ
                    close = not known(n) or 1 <= n <= NQ
                    q = 1 - p
                    t1 = n * AG + (half * T + AG)
                    if prep:
                        if not known(n) or n + B >= 0:
                            dve.wait_ge(s_xnp, n + (B + 1))
                        for a in range(AG):
                            if known(n):
                                tt = (n + 1) * AG + a
                            ins = dve.tensor_scalar(
                                xn[:, a, :], X[:, half * T + tt, :] if known(n) else X[:, bass.ds(t1 + a, 1), :],
                                mean(n, a), rs(n, a), ALU.subtract, ALU.mult)
                        ins.then_inc(s_xn, 1)
                    if known(n) and n - 1 in inside:
                        logits(*inside[n - 1], bank[5])
                    if core:
                        mask(n, 0)
                    if known(n) and n in route:
                        route_picks(route[n])
                    if not known(n) or 2 <= n < NQ + 2:
                        dve.wait_ge(s_o, n + (B - 1))
                        t0 = n * AG + (half * T - 2 * AG)
                        xg = X[:, bass.ds(t0, AG), :]
                        dve.tensor_tensor(xg, xg, bank[7][:, 0:AT].rearrange("p (a c) -> p a c", a=AG),
                                          ALU.add).then_inc(s_xa, 1)
                    if prep:
                        dve.wait_ge(s_XT, n + (B + 2))
                        dve.tensor_tensor(delta[:], xT[:, q, 1:AT + 1], xT[:, q, 0:AT], ALU.subtract).then_inc(s_delta, 1)
                        dve.wait_ge(s_delta, n + (B + 2))
                        if not known(n) or n + B >= 0:
                            dve.wait_ge(s_kp, n + (B + 1))
                        for i, m in enumerate("rkvg"):
                            ins = dve.scalar_tensor_tensor(mix[:, i, :], delta[:], col("mix_" + m), xT[:, q, 0:AT],
                                                           ALU.mult, ALU.add)
                        ins.then_inc(s_mix, 1)
                    if core:
                        update(n, 0)
                    if close:
                        group_norm(n, q)
                    if known(n) and n in inside:
                        add_proj(*inside[n], bank[5])
                    if known(n) and n in route:
                        route_counts(route[n], bank[5])
                    if core:
                        mask(n, 1)
                    if known(n) and n in inside:
                        norm2_apply(*inside[n])
                    if prep:
                        dve.wait_ge(s_rk, n + (B + 2))
                        r = rT[:]
                        for l in range(HQ):
                            dve.tensor_scalar(rx[:, q, :, l, :], r, const("heads4")[:, l:l + 1], None, ALU.mult)
                        dve.tensor_tensor(rw[:, q], r, w_since[:].unsqueeze(1).broadcast_to([P, AG, P]),
                                          ALU.mult).then_inc(s_rx, 1)
                        dve.wait_ge(s_kp, n + (B + 2))
                        dve.tensor_tensor(kw[:, q], bank[7][:, 0:AT].rearrange("p (a c) -> p a c", a=AG),
                                          w_until[:].unsqueeze(1).broadcast_to([P, AG, C]), ALU.mult).then_inc(s_kw, 1)
                    if core:
                        update(n, 1)
                    if known(n) and n in route:
                        route_slots(route[n])
                    if half == 0 and known(n) and NQ - 2 <= n < NQ - 2 + G:
                        combine_stats(1, n - (NQ - 2))
                    if known(n) and n + 1 in inside:
                        if inside[n + 1][0] % 2 == half:
                            dve.wait_ge(s_xa, B + 2 * inside[n + 1][1] + 2)
                        norm_stats(*inside[n + 1])
                        norm_apply(*inside[n + 1])

                def mean(n, a):
                    return amv[:, half, bass.ds(n * AG + (AG + a), 1), 0]

                def rs(n, a):
                    return arstd[:, half, bass.ds(n * AG + (AG + a), 1)]

                attention_steps(dve, NQ + 1, inside, step)

            link.step(dve.memset(ones_et[:], 1.0))
            dve.memset(kz[:], 0.0).then_inc(s_kz, 1)
            link.wait()
            link.step(dve.memset(ones_et[:, :, 0:1], 0.0))
            dve.wait_ge(s_small, 16 * 6)
            fronts()
            tables()
            experts(0)
            experts(1, after=lambda g: combine_stats(0, g))
            attention(0)
            attention(1, INSIDE, ROUTE)
            experts(2)
            experts(3, after=lambda g: combine(2, g))
            for g in range(G):
                combine(3, g)

        @block.tensor
        def _(pe):
            def fronts():
                for s in range(1, HALVES * G + 4):
                    if 0 <= s - 2 < HALVES * G:
                        m = s - 2
                        if m >= 2:
                            pe.wait_ge(s_h, m - 1)
                        project(m, bank[2 + m % 2])
                    if 0 <= s - 1 < HALVES * G:
                        m = s - 1
                        if m >= 2:
                            pe.wait_ge(s_n1T, m - 1)
                        n1_turn(m, bank[m % 2])
                    if 0 <= s - 4 < HALVES * G:
                        m = s - 4
                        if m >= 1:
                            pe.wait_ge(s_logc, m)
                        gate_logits(m, bank[6])
                    if 0 <= s - 3 < HALVES * G:
                        m = s - 3
                        if m >= 2:
                            pe.wait_ge(s_n2T, m - 1)
                        n2_turn(m, bank[4 + m % 2])
                    if s - 3 in (G, 2 * G):
                        run = (s - 3) // G - 1
                        if run:
                            pe.wait_ge(s_cntc, run)
                        count(run, bank[7])

            def n1_turn(m, dst):
                pe.wait_ge(s_n1, m + 1)
                for t in range(GROUP):
                    mm = pe.transpose(dst[:, t * P:(t + 1) * P], n1[:, m % 2, t, :], ident)
                mm.then_inc(s_n1p, 1)

            def project(m, dst):
                pe.wait_ge(s_n1T, m + 1)
                for t in range(GROUP):
                    mm = pe.matmul(dst[:, t * C:(t + 1) * C], n1T[:, m % 2, t * P:(t + 1) * P],
                                   weight("proj"), start=True, stop=True)
                mm.then_inc(s_proj, 1)

            def n2_turn(m, dst):
                pe.wait_ge(s_n2, m + 1)
                half, s = RUNS[m // G][1], m % G
                for t in range(GROUP):
                    mm = pe.transpose(dst[:, t * P:(t + 1) * P], n2[half][:, s * GROUP + t, :], ident)
                mm.then_inc(s_n2p, 1)

            def gate_logits(m, dst):
                pe.wait_ge(s_n2T, m + 1)
                for t in range(GROUP):
                    mm = pe.matmul(dst[:, t * E:(t + 1) * E], n2T[:, m % 2, t * P:(t + 1) * P],
                                   gate[:], start=True, stop=True)
                mm.then_inc(s_logit, 1)

            def count(run, dst):
                pe.wait_ge(s_pick, run + 1)
                flat = both[:].rearrange("p t e -> p (t e)")
                pe.matmul(dst[:, 0:T * E], const("before"), flat, start=True, stop=True)
                pe.matmul(dst[:, T * E:2 * T * E], const("ones"), flat, start=True, stop=True
                          ).then_inc(s_count, 1)

            def experts(run):
                layer, half = RUNS[run]
                base = run * NXT
                pe.wait_ge(s_table, run + 1)
                if run == 0:
                    pe.wait_ge(s_big, 16 * 3)

                def step(n, k):
                    k2 = (base + k) % 2
                    k4 = (base + k + 1) % 4
                    if not known(n) or n + 1 < NXT:
                        if known(n):
                            pe.wait_ge(s_load[k4], 16 * ((base + n + 1) // 4 + 1))
                        else:
                            pe.wait_ge(s_load[k4], n * 4 + (4 * (base + 1 - k4) + 16))
                        if not known(n) or n + base >= 0:
                            pe.wait_ge(s_xT, n + (base + 1))
                        pe.transpose(bank[0][:, 0:P], xs[:, k4, :], ident).then_inc(s_xp, 1)
                    if not known(n) or 0 <= n < NXT:
                        at = pe.value_load(tile_e[0:1, half, bass.ds(n, 1)], min_val=0, max_val=(E - 1) * INTER)
                        pe.wait_ge(s_xT, n + (base + 1))
                        if not known(n) or base + n >= 2:
                            pe.wait_ge(s_hid, n + (base - 1))
                        pe.matmul(bank[1 + k2][:], xsT[:, k2, :], wg[:, bass.ds(at, INTER)], start=True, stop=True)
                        pe.matmul(bank[3 + k2][:], xsT[:, k2, :], wu[:, bass.ds(at, INTER)], start=True, stop=True
                                  ).then_inc(s_gu, 1)
                    if not known(n) or 1 <= n < NXT + 1:
                        pe.wait_ge(s_hid, n + base)
                        if not known(n) or base + n - 1 >= 2:
                            pe.wait_ge(s_hT, n + (base - 2))
                        for c in range(CH):
                            mm = pe.transpose(bank[5 + (1 - k2)][:, c * P:(c + 1) * P],
                                              hid[:, 1 - k2, c * P:(c + 1) * P], ident)
                        mm.then_inc(s_hp, 1)
                    if not known(n) or 2 <= n < NXT + 2:
                        at = pe.value_load(tile_e[0:1, half, bass.ds(n - 2, 1)], min_val=0, max_val=(E - 1) * INTER)
                        pe.wait_ge(s_hT, n + (base - 1))
                        if not known(n) or base + n - 2 >= 1:
                            pe.wait_ge(s_yc, n + (base - 2))
                        for c in range(CH):
                            mm = pe.matmul(bank[7][:, 0:C], hidT[:, k2, c * P:(c + 1) * P],
                                           wd[:, bass.ds(at + c * P, C)], start=(c == 0), stop=(c == CH - 1))
                        mm.then_inc(s_y, 1)

                steps(pe, -1, LO, HI, NXT + 1, UN, step)

            def attention(half, inside={}, route={}):
                B = half * NQ
                if half == 0:
                    pe.wait_ge(s_yc, 2 * NXT)

                def scores(n, p, c, quads):
                    for q in quads:
                        if not known(n) or c or n >= 1:
                            pe.wait_ge(s_att, n * 8 + (8 * B + 4 * c + q - 3))
                        pe.matmul(bank[q][:], kz[:, p, q, c * P:(c + 1) * P],
                                  rx[:, p, c].rearrange("p l i -> p (l i)"),
                                  start=True, stop=True).then_inc(s_sc, 1)

                def chunk_kv(n, p, c):
                    if not known(n) or c or n >= 1:
                        pe.wait_ge(s_add, n * 2 + (2 * B + c))
                    pe.matmul(bank[5][:, 0:C], kw[:, p, c, :], v_own(p, c), start=True, stop=True
                              ).then_inc(s_kv, 1)

                def chunk_out(n, p, c):
                    if c == 0 and (not known(n) or n >= 1):
                        pe.wait_ge(s_y8, n + B)
                        pe.wait_ge(s_yroot, n + B)
                    if not known(n) or c or n >= 1:
                        pe.wait_ge(s_state, n * 2 + (2 * B + c))
                    pe.matmul(bank[4][:, c * P:(c + 1) * P], state[:, c, :], rw[:, p, c, :], start=True, stop=False,
                              skip_group_check=True)
                    pe.wait_ge(s_att, n * 8 + (8 * B + 4 * c + 4))
                    for l in range(HQ):
                        for q in range(QUADS):
                            mm = pe.matmul(bank[4][32 * q:32 * q + 32, c * P:(c + 1) * P],
                                           vz[:, p, c, q, 32 * l:32 * l + 32], att[:, c, q * HQ + l, :],
                                           start=False, stop=(l == HQ - 1), skip_group_check=True)
                    mm.then_inc(s_av, 1)

                def step(n, p):
                    prep = not known(n) or n + 1 < NQ
                    core = not known(n) or 0 <= n < NQ
                    close = not known(n) or 1 <= n <= NQ
                    q = 1 - p
                    if core:
                        pe.wait_ge(s_rx, n + (B + 1))
                        scores(n, p, 0, (0, 1))
                    if close:
                        pe.wait_ge(s_y8, n + B)
                        pe.matmul(bank[4][:, AT:2 * AT], const("centre"), yT[:], start=True, stop=True
                                  ).then_inc(s_cen, 1)
                    if core:
                        scores(n, p, 0, (2, 3))
                    if close:
                        pe.wait_ge(s_sq, n + B)
                        pe.matmul(bank[4][:, 0:AT], const("average"), sq[:], start=True, stop=True
                                  ).then_inc(s_yvar, 1)
                    if prep:
                        pe.wait_ge(s_xn, n + (B + 2))
                        if not known(n) or n + B >= 0:
                            pe.wait_ge(s_vg, n + (B + 1))
                        for a in range(AG):
                            mm = pe.transpose(bank[6][:, a * P:(a + 1) * P], xn[:, a, :], ident)
                        mm.then_inc(s_xnp, 1)
                    if not known(n) or 2 <= n < NQ + 2:
                        pe.wait_ge(s_z, n + (B - 1))
                        if not known(n) or n < NQ:
                            pe.wait_ge(s_kw, n + (B + 1))
                        elif n > NQ:
                            pe.wait_ge(s_xa, n + (B - 2))
                        for a in range(AG):
                            mm = pe.matmul(bank[7][:, a * C:(a + 1) * C], zT[:, a * P:(a + 1) * P], weight("o"),
                                           start=True, stop=True)
                        mm.then_inc(s_o, 1)
                    fm = group_no(inside[n]) if known(n) and n in inside else None
                    kv_read = 2 * B + 2 * min(n, NQ) if known(n) else None
                    if fm is not None:
                        if kv_read:
                            pe.wait_ge(s_add, kv_read)
                        pe.wait_ge(s_logc, fm)
                        pe.wait_ge(s_cntc, fm // G)
                        n1_turn(fm, bank[5])
                    if core:
                        pe.wait_ge(s_kw, n + (B + 1))
                        pe.wait_ge(s_vg, n + (B + 1))
                        if fm is not None:
                            pe.wait_ge(s_n1T, fm + 1)
                        elif known(n) and n - 1 in inside:
                            pe.wait_ge(s_logc, group_no(inside[n - 1]) + 1)
                        chunk_kv(n, p, 0)
                        chunk_out(n, p, 0)
                        kv_read = 2 * B + 2 * n + 1 if known(n) else None
                    if fm is not None:
                        pe.wait_ge(s_add, kv_read)
                        project(fm, bank[5])
                    if known(n) and n in route:
                        pe.wait_ge(s_add, kv_read)
                        pe.wait_ge(s_logc, (route[n] + 1) * G)
                        count(route[n], bank[5])
                    if prep:
                        pe.wait_ge(s_mix, n + (B + 2))
                        if not known(n) or n >= 2:
                            pe.wait_ge(s_xa, n + (B - 1))
                        elif n >= 0:
                            pe.wait_ge(s_kw, n + (B + 1))
                        for i, m in enumerate("rk"):
                            mm = pe.matmul(bank[7][:, i * AT:(i + 1) * AT], weight(m), mix[:, i, :],
                                           start=True, stop=True)
                        mm.then_inc(s_rkp, 1)
                    if core:
                        scores(n, p, 1, range(QUADS))
                    if prep:
                        pe.wait_ge(s_XT, n + (B + 2))
                        for a in range(AG):
                            pe.matmul(bank[6][:, a * C:(a + 1) * C], mix[:, 2, a * P:(a + 1) * P], weight("v"),
                                      start=True, stop=True)
                        mm = pe.matmul(bank[6][:, AT:2 * AT], weight("g"), mix[:, 3, :], start=True, stop=True)
                        mm.then_inc(s_vgp, 1)
                        pe.wait_ge(s_rk, n + (B + 2))
                        for a in range(AG):
                            mm = pe.matmul(bank[7][:, a * C:(a + 1) * C], mix[:, 1, a * P:(a + 1) * P], weight("k"),
                                           start=True, stop=True)
                        mm.then_inc(s_kp, 1)
                    if fm is not None:
                        pe.wait_ge(s_h, fm + 1)
                        n2_turn(fm, bank[5])
                    if core:
                        if fm is not None:
                            pe.wait_ge(s_n2T, fm + 1)
                        if known(n) and n in route:
                            pe.wait_ge(s_cntc, route[n] + 1)
                        chunk_kv(n, p, 1)
                        chunk_out(n, p, 1)
                        kv_read = 2 * B + 2 * n + 2 if known(n) else None
                    if fm is not None:
                        pe.wait_ge(s_add, kv_read)
                        gate_logits(fm, bank[5])
                attention_steps(pe, NQ + 1, inside, step)

            pe.wait_ge(s_small, 16 * 6)
            fronts()
            experts(0)
            experts(1)
            attention(0)
            attention(1, INSIDE, ROUTE)
            experts(2)
            experts(3)


def _constants():
    import numpy as np
    c = np.zeros((P, NCONST), np.float32)
    p = np.arange(P)

    def put(name, v):
        a, b = CONST[name]
        c[:, a:b] = v
    put("ident", np.eye(P))
    put("before", p[:, None] < p[None, :])
    put("ones", 1.0)
    put("later", p[None, :] > p[:, None])
    put("gap", np.maximum(p[None, :] - p[:, None] - 1, 0))
    put("iota", p[None, :])
    put("block", p[:, None] // HD == p[None, :] // HD)
    put("centre", np.eye(P) - (p[:, None] // HD == p[None, :] // HD) / HD)
    put("average", (p[:, None] // HD == p[None, :] // HD) / HD)
    put("eps", EPS)
    put("heads4", (p[:, None] // HD) % HQ == np.arange(HQ)[None, :])
    put("left", (P - 1 - p)[:, None])
    put("rank", (E - np.arange(E))[None, :])
    put("limit", (P * np.arange(T))[None, :])
    put("tile", np.arange(XT + 1)[None, :])
    return c


def kernel(**inputs):
    import numpy as _np
    import concourse.bacc as _bacc
    from concourse import mybir as _mybir
    from concourse.bass_utils import run_bass_kernel_spmd as _run

    def get(name):
        return _np.asarray(inputs["L0_" + name])

    ffn, attn = "ffn_", "attn_"
    decay = _np.repeat(get("attn_time_decay"), HD)
    arrays = {
        "x": get("attn_xq").reshape(HALVES * SEQ, C),
        "consts": _constants(),
        "cols": _np.stack([get("ffn_ln1_g"), get("ffn_ln1_b"), get("ffn_ln2_g"), get("ffn_ln2_b")]
                          + [get("attn_time_mix_" + m).reshape(C) for m in "rkvg"]
                          + [decay, get("attn_ln_w"), get("attn_ln_b")], axis=1),
        "rows": _np.stack([_np.broadcast_to(decay[None, :], (P, C))], axis=1),
        "bonus": _np.broadcast_to(get("attn_time_faaaa")[None, :], (P, HEADS)),
        "weights": _np.stack([get("ffn_attn_w").T] + [get("attn_W_" + m).T for m in "rkvgo"], axis=1),
        "gate": get("ffn_gate_w").T,
        "wg": get("ffn_gate_proj").transpose(2, 0, 1).reshape(C, E * INTER),
        "wu": get("ffn_up_proj").transpose(2, 0, 1).reshape(C, E * INTER),
        "wd": get("ffn_down_proj").reshape(E, C, CH, P).transpose(3, 0, 2, 1).reshape(P, E * INTER),
    }
    nc = _bacc.Bacc("TRN2", target_bir_lowering=False, num_devices=1)
    launch, args = {}, []
    for name, a in arrays.items():
        a = _np.ascontiguousarray(a)
        launch[f"in_{name}"] = a
        args.append(nc.dram_tensor(f"in_{name}", a.shape, _mybir.dt.from_np(a.dtype), kind="ExternalInput").ap())
    out = nc.dram_tensor("out_x", (HALVES * SEQ, C), F32, kind="ExternalOutput").ap()
    macaron(nc, *args, out)
    r = _run(nc, [launch], core_ids=[0])
    return r.results[0]["out_x"].reshape(HALVES, SEQ, C)
```

```python
from contextlib import ExitStack

import concourse.bass as bass
from concourse import mybir

F32 = mybir.dt.float32
F32R = mybir.dt.float32r
I32 = mybir.dt.int32
ALU = mybir.AluOpType
ACT = mybir.ActivationFunctionType
AX = mybir.AxisListType.X

P = 128
C = 128
HALVES = 2
SEQ = 2048
T = SEQ // P
GROUP = 4
G = T // GROUP
E = 8
INTER = 512
CH = INTER // P
TOP = 2
HEADS = 16
HD = C // HEADS
HQ = 32 // HD
EPS = 1e-5
XT = (SEQ * TOP + E * (P - 1)) // P
SLOTS = XT * P
FILL = 3
BIG = 3.0e38
DECAY_MAX = 1.0e30
AG = 2
AT = AG * P
NQ = T // AG
QUADS = C // 32
NA = HALVES * NQ
VQ = HQ * (32 + HD)

CONST = {}
_at = 0
for _name, _width in (("ident", P), ("before", P), ("ones", P), ("later", P), ("gap", P), ("iota", P),
                      ("block", P), ("centre", P), ("average", P), ("eps", 1), ("heads4", HQ), ("left", 1),
                      ("rank", E), ("limit", T), ("tile", XT)):
    CONST[_name] = (_at, _at + _width)
    _at += _width
NCONST = _at
COLS = ("ln1_g", "ln1_b", "ln2_g", "ln2_b", "mix_r", "mix_k", "mix_v", "mix_g", "decay", "ln_w", "ln_b")
ROWS = ("decay",)
WEIGHTS = ("proj", "r", "k", "v", "g", "o")

SECOND_LATE = 3

STATS = {6: 0, 8: 1, 10: 2, 12: 3}
FRONT = {7: (2, 0), 8: (2, 1), 9: (2, 2), 10: (2, 3), 13: (3, 0), 14: (3, 1), 15: (3, 2)}
FRONT_END = {n + 1: front for n, front in FRONT.items()}
ROUTE = {11: 2}
LAST_FRONT = (3, 3)
PE_PARTS = {0: "n1_turn", 1: "project", 4: "n2_turn", 5: "logits", 7: "count"}
ACT_PARTS = {0: "n1_out", 2: "roots2", 3: "n2_rows", 4: "n2_out", 7: "top_exp"}
DVE_PARTS = {1: "add_proj", 2: "scale", 5: "logits", 6: "picks", 7: "counts", 9: "slots"}


def rows_ready(run, g):
    return run % HALVES * NQ + (g + 1) * GROUP // AG


def early(n):
    return rows_ready(*FRONT[n]) <= n - 2


class Chain:

    def __init__(self, eng, sem, base=0):
        self.eng, self.sem, self.base, self.n = eng, sem, base, 0

    def step(self, ins):
        ins.then_inc(self.sem, 1)
        self.n += 1

    def wait(self):
        if self.base + self.n:
            self.eng.wait_ge(self.sem, self.base + self.n)


def steps(eng, first, loops, last, unroll, step):
    n = first
    for lo, hi in loops:
        assert (hi - lo) % unroll == 0
        for m in range(n, lo):
            step(m, m % unroll)
        with eng.Fori(0, (hi - lo) // unroll) as i:
            for k in range(unroll):
                step(i * unroll + (lo + k), (lo + k) % unroll)
        n = hi
    for m in range(n, last + 1):
        step(m, m % unroll)


def attention_steps(eng, step):
    steps(eng, -1, ((2, 6),), NA + 1, 2, step)


def group_no(group):
    return group[0] * G + group[1]


def front_steps():
    begin = {m + (m >= G) * SECOND_LATE: m for m in range(HALVES * G)}
    for s in range(HALVES * G + SECOND_LATE + 5):
        yield [begin.get(s - age) for age in range(6)]


def known(n):
    return isinstance(n, int)


def macaron(nc, x_in, consts_in, cols_in, rows_in, bonus_in, weights_in, gate_in, wg_in, wu_in, wd_in, out):
    with ExitStack() as ctx:
        def sb(name, shape, dt=F32):
            return ctx.enter_context(nc.sbuf_tensor(name, shape, dt))

        def sem(name):
            return ctx.enter_context(nc.semaphore(name))

        bank = [ctx.enter_context(nc.psum_tensor(f"bank{i}", [P, 512], F32)) for i in range(8)]

        X = sb("X", [P, HALVES * T, C])
        H = sb("H", [P, HALVES * T, C])
        consts = sb("consts", [P, NCONST])
        cols = sb("cols", [P, len(COLS)])
        rows = sb("rows", [P, len(ROWS), C])
        bonus = sb("bonus", [P, HEADS])
        weights = sb("weights", [P, len(WEIGHTS), C])
        gate = sb("gate", [P, E])
        w_hi = sb("w_hi", [P, 2, E * INTER], F32R)
        wd = sb("wd", [P, E * INTER])

        def const(name):
            a, b = CONST[name]
            return consts[:, a:b]

        def col(name):
            i = COLS.index(name)
            return cols[:, i:i + 1]

        def row(name):
            return rows[:, ROWS.index(name), :]

        def weight(name):
            return weights[:, WEIGHTS.index(name), :]

        ident = const("ident")

        mv = sb("mv", [P, 2, GROUP, 2])
        bn = sb("bn", [P, GROUP, 6])
        var2 = sb("var2", [P, 2, 2, GROUP])
        root = sb("root", [P, 2, 2, GROUP])
        rstd = sb("rstd", [P, 2, 2, GROUP])
        shift = sb("shift", [P, 2, GROUP])
        shift2 = sb("shift2", [P, 2, GROUP])
        mv2 = sb("mv2", [P, 2, GROUP, 2])
        root2 = sb("root2", [P, 2, GROUP])
        rstd2 = sb("rstd2", [P, 2, GROUP])
        n1 = sb("n1", [P, 2, GROUP, C])
        n2T = sb("n2T", [P, 2, GROUP * P])
        L = sb("L", [P, T, E])
        L2 = sb("L2", [P, T, E])
        eq = sb("eq", [P, T, E])
        pick = sb("pick", [P, TOP, T, E])
        both = sb("both", [P, T, E])
        best = sb("best", [P, TOP, T])
        first = sb("first", [P, T])
        gap2 = sb("gap2", [P, T])
        wexp = sb("wexp", [P, T])
        wden = sb("wden", [P, T])
        share = sb("share", [P, HALVES, TOP, T])
        counts = sb("counts", [P, E, T])
        ahead = sb("ahead", [P, T, E])
        cum = sb("cum", [P, E, T])
        ones_et = sb("ones_et", [P, E, T])
        over = sb("over", [P, E, T])
        tiles_e = sb("tiles_e", [P, E])
        ends = sb("ends", [P, E])
        start = sb("start", [P, E])
        slot_e = sb("slot_e", [P, T, E])
        slot_f = sb("slot_f", [P, TOP, T])
        slot = sb("slot", [P, HALVES, TOP, T], I32)
        done_e = sb("done_e", [P, XT, E])
        tile_ef = sb("tile_ef", [P, XT])
        tile_e = sb("tile_e", [P, HALVES * XT], I32)
        slots_io = sb("slots_io", [P, 8 * C])
        xs = slots_io[:, 0:4 * C].rearrange("p (k c) -> p k c", k=4)
        ys = slots_io[:, 4 * C:8 * C].rearrange("p (k c) -> p k c", k=4)
        mix = slots_io[:].rearrange("p (m i) -> p m i", m=4)
        xsT = sb("xsT", [P, 2, P])
        x_hi = sb("x_hi", [P, 2, P], F32R)
        x_lo = sb("x_lo", [P, 2, P], F32R)
        shared = sb("shared", [P, 2 * HEADS * P])
        sg, hid, hidT, n1T = (shared[:, i * 2 * INTER:(i + 1) * 2 * INTER].rearrange("p (b i) -> p b i", b=2)
                         for i in range(4))
        att = shared[:].rearrange("p (b h i) -> p b h i", b=2, h=HEADS)
        Y = sb("Y", [P, TOP, T, C])
        n2a = sb("n2a", [P, T, C])
        n2 = (n2a[:], Y[:, 1])
        zero = Y[:, 0, 0:SLOTS // FILL // P, :]

        swap = sb("swap", [P, 2 * E * INTER])
        w_lo = swap[:].bitcast(F32R).rearrange("p (m i) -> p m i", m=2)
        swap_at = [0]

        def part(width):
            swap_at[0] += width
            return swap[:, swap_at[0] - width:swap_at[0]]

        kz = part(2 * QUADS * AT).rearrange("p (b q i) -> p b q i", b=2, q=QUADS)
        rx = part(2 * AG * HQ * P).rearrange("p (b a l i) -> p b a l i", b=2, a=AG, l=HQ)
        assert swap_at[0] == E * INTER
        vz = part(2 * AG * QUADS * VQ).rearrange("p (b a q v) -> p b a q v", b=2, a=AG, q=QUADS)
        kw = part(2 * AG * C).rearrange("p (b a c) -> p b a c", b=2, a=AG)
        rw = part(2 * AG * P).rearrange("p (b a i) -> p b a i", b=2, a=AG)
        rT = part(AG * P).rearrange("p (a i) -> p a i", a=AG)
        delta = part(AT)
        assert swap_at[0] == 2 * E * INTER
        wm = sb("wm", [P, HEADS, P])
        negd_col = sb("negd_col", [P, 1])
        expd_col = sb("expd_col", [P, 1])
        expd_row = sb("expd_row", [P, C])
        negd_row = sb("negd_row", [P, C])
        w_chunk = sb("w_chunk", [P, 1])
        w_since = sb("w_since", [P, P])
        w_until = sb("w_until", [P, C])
        amv = sb("amv", [P, HALVES * T, 2])
        abn = sb("abn", [P, T, 6])
        aroot = sb("aroot", [P, HALVES * T])
        arstd = sb("arstd", [P, HALVES * T])
        xn = sb("xn", [P, AG, C])
        xT = sb("xT", [P, 2, AT + 1])
        gT = sb("gT", [P, 2, AT])
        state = sb("state", [P, 2, C])
        add = sb("add", [P, AG, C])
        yT = sb("yT", [P, AT])
        yc = sb("yc", [P, AT])
        sq = sb("sq", [P, AT])
        yn = sq
        yroot = sb("yroot", [P, AT])
        zT = sb("zT", [P, AT])

        lo_store = [nc.dram_tensor(f"lo_store{m}", (P, E * INTER), F32, kind="Internal").ap() for m in range(2)]
        slot_rows = [nc.dram_tensor(f"slot_rows{h}", (SLOTS, C), F32, kind="Internal").ap() for h in range(HALVES)]
        y_rows = [nc.dram_tensor(f"y_rows{h}", (SLOTS, C), F32, kind="Internal").ap() for h in range(HALVES)]

        s_x = [sem(f"x_loaded{g}") for g in range(HALVES * G)]
        s_small = sem("small_loaded")
        s_gu_in = [sem(f"{m}_weights_loaded") for m in ("gate", "up")]
        s_hi = sem("weights_high_ready")
        s_lo = sem("weights_low_ready")
        s_lo_out = sem("weights_low_stored")
        s_lo_in = [sem(f"{m}_weights_low_loaded") for m in ("gate", "up")]
        s_xlo = sem("x_low_ready")
        s_down_in = sem("down_weights_loaded")
        s_zero = sem("zero_ready")
        s_filled = sem("slots_filled")
        s_dve = sem("vector_step")
        s_pool = sem("gpsimd_step")
        s_var = sem("variances")
        s_root = sem("roots")
        s_n1 = sem("n1_ready")
        s_n1p = sem("n1_transposed")
        s_n1T = sem("n1T_ready")
        s_proj = sem("proj_done")
        s_var2 = sem("variances2")
        s_root2 = sem("roots2")
        s_n2 = sem("n2_ready")
        s_n2p = sem("n2_transposed")
        s_n2T = sem("n2T_ready")
        s_logit = sem("logits_done")
        s_h = sem("h_ready")
        s_cntc = sem("counts_copied")
        s_logc = sem("logits_copied")
        s_gap = sem("top_gap_ready")
        s_exp = sem("top_exp_ready")
        s_pick = sem("picks_ready")
        s_count = sem("counts_done")
        s_table = sem("slots_ready")
        s_scat = [sem(f"rows_scattered{h}") for h in range(HALVES)]
        s_load = [sem(f"slot_rows_loaded{k}") for k in range(4)]
        s_xp = sem("xs_transposed")
        s_xT = sem("xsT_ready")
        s_gu = sem("gate_up_done")
        s_sg = sem("silu_ready")
        s_hid = sem("hidden_ready")
        s_hp = sem("hidden_transposed")
        s_hT = sem("hiddenT_ready")
        s_y = sem("down_done")
        s_yc = sem("y_copied")
        s_store = [sem(f"y_stored{k}") for k in range(4)]
        s_got = [sem(f"y_gathered{g}") for g in range(G)]
        s_comb = sem("combined")
        s_out = sem("output_stored")

        s_tab = sem("decay_tables_step")
        s_tabv = sem("decay_tables_ready")
        s_avar = sem("attn_variances")
        s_aroot = sem("attn_roots")
        s_xn = sem("xn_ready")
        s_xnp = sem("xn_transposed")
        s_XT = sem("XT_ready")
        s_delta = sem("delta_ready")
        s_mix = sem("mix_ready")
        s_rkp = sem("rk_projected")
        s_kz = sem("k_zeroed")
        s_rk = sem("rk_ready")
        s_vgp = sem("vg_projected")
        s_vg = sem("vg_ready")
        s_kp = sem("k_rows_projected")
        s_kw = sem("kw_ready")
        s_rx = sem("rx_ready")
        s_rw = sem("rw_ready")
        s_hn = sem("h_normalized")
        s_rstd2 = sem("rstd2_ready")
        s_sc = sem("scores_done")
        s_att = sem("att_ready")
        s_kv = sem("kv_done")
        s_add = sem("kv_masked")
        s_state = sem("state_ready")
        s_av = sem("chunk_output_done")
        s_y8 = sem("chunk_outputs_copied")
        s_vz = sem("v_padding_zeroed")
        s_cen = sem("centred")
        s_sq = sem("squared")
        s_yvar = sem("head_variances")
        s_yroot = sem("head_roots")
        s_yrstd = sem("head_rstd_ready")
        s_yn = sem("normalized")
        s_z = sem("z_ready")
        s_o = sem("attn_out_done")
        s_xa = sem("attn_added")

        block = ctx.enter_context(nc.Block())
        RUNS = [(0, 0), (0, 1), (1, 0), (1, 1)]
        TILES = HALVES * XT

        UN = 4
        LO, MID, HI = (3, 11), (XT - 4, XT + 4), TILES - 3
        ROOTS = HI
        COMBINED = HI - 8

        def v_own(q, a):
            return vz[:, q, a].rearrange("p q (l x) -> p q l x", l=HQ)[:, :, :, 0:HD]

        @block.sync
        def _(sp):
            sp.dma_start(consts[:], consts_in).then_inc(s_small, 16)
            sp.dma_start(cols[:], cols_in).then_inc(s_small, 16)
            sp.dma_start(weights[:], weights_in).then_inc(s_small, 16)
            sp.dma_start(gate[:], gate_in).then_inc(s_small, 16)
            sp.dma_start(rows[:], rows_in).then_inc(s_small, 16)
            sp.dma_start(bonus[:], bonus_in).then_inc(s_small, 16)
            for g in range(HALVES * G):
                sp.dma_start(X[:, g * GROUP:(g + 1) * GROUP, :],
                             x_in[g * GROUP * P:(g + 1) * GROUP * P, :].rearrange("(t p) c -> p t c", p=P)
                             ).then_inc(s_x[g], 16)
            for m, src in enumerate((wg_in, wu_in)):
                sp.dma_start(swap[:, m * E * INTER:(m + 1) * E * INTER], src).then_inc(s_gu_in[m], 16)
            sp.wait_ge(s_zero, 1)
            for h in range(HALVES):
                for q in range(FILL):
                    n = SLOTS // FILL
                    sp.dma_start(slot_rows[h][q * n:(q + 1) * n, :].rearrange("(p a) c -> p a c", p=P),
                                 zero).then_inc(s_filled, 16)
            sp.dma_start(wd[:], wd_in).then_inc(s_down_in, 16)
            for m in range(2):
                sp.wait_ge(s_lo, m + 1)
                sp.dma_start(lo_store[m], swap[:, m * E * INTER:(m + 1) * E * INTER]).then_inc(s_lo_out, 16)

            for layer in range(2):
                base = layer * TILES

                def place(n):
                    half = n // XT if known(n) else second
                    return half, n * P + (-half * SLOTS)

                def load(n, k):
                    if not known(n) or base + n >= 4:
                        sp.wait_ge(s_xp, n + (base - 3))
                    half, at = place(n)
                    sp.dma_start(xs[:, k, :], slot_rows[half][bass.ds(at, P), :]).then_inc(s_load[k], 16)

                def store(n, k):
                    sp.wait_ge(s_yc, n + (base + 1))
                    half, at = place(n)
                    sp.dma_start(y_rows[half][bass.ds(at, P), :], ys[:, k, :]).then_inc(s_store[k], 16)

                def step(n, k):
                    if known(n) and n in (0, XT):
                        sp.wait_ge(s_scat[n // XT], 16 * TOP * T * (layer + 1))
                    if known(n) and n == 0 and layer:
                        sp.wait_ge(s_lo_out, 16 * 2)
                        sp.wait_ge(s_sc, 8 * NA)
                        sp.dma_start(swap[:, 0:E * INTER], lo_store[0]).then_inc(s_lo_in[0], 16)
                        sp.wait_ge(s_kp, NA)
                    if not known(n) or n < TILES:
                        load(n, (base + k) % 4)
                    if not known(n) or n >= 5:
                        store(n - 5, (base + k - 5) % 4)

                second = 0
                steps(sp, 0, ((5, XT - 2),), XT + 5, UN, step)
                second = 1
                steps(sp, XT + 6, ((XT + 6, TILES - 5),), TILES + 4, UN, step)
            for half in range(HALVES):
                for g in range(G):
                    sp.wait_ge(s_comb, (2 + half) * G + g + 1)
                    t = half * T + g * GROUP
                    sp.dma_start(out[t * P:(t + GROUP) * P, :].rearrange("(t p) c -> p t c", p=P),
                                 X[:, t:t + GROUP, :]).then_inc(s_out, 16)
            sp.wait_ge(s_out, 16 * HALVES * G)

        @block.gpsimd
        def _(pool):
            link = Chain(pool, s_pool)
            pool.memset(zero, 0.0).then_inc(s_zero, 1)

            def scatter(run):
                layer, half = RUNS[run]
                if layer == 0:
                    pool.wait_ge(s_filled, 16 * FILL * HALVES)
                pool.wait_ge(s_table, run + 1)
                for t in range(T):
                    for k in range(TOP):
                        pool.indirect_dma_start(
                            slot_rows[half], bass.IndirectOffsetOnAxis(slot[:, half, k, t:t + 1], 0),
                            n2[half][:, t, :], None).then_inc(s_scat[half], 16)

            def gather(run):
                layer, half = RUNS[run]
                for k in range(4):
                    pool.wait_ge(s_store[k], 16 * len([n for n in range((run + 1) * XT) if n % 4 == k]))
                if run:
                    pool.wait_ge(s_comb, run * G)
                pool.wait_ge(s_scat[1], 16 * TOP * T * (layer + 1))
                for t in range(T):
                    for k in range(TOP):
                        pool.indirect_dma_start(
                            Y[:, k, t, :], None, y_rows[half],
                            bass.IndirectOffsetOnAxis(slot[:, half, k, t:t + 1], 0)
                        ).then_inc(s_got[t // GROUP], 16)

            def combine(run, g):
                layer, half = RUNS[run]
                t0 = half * T + g * GROUP
                xg = X[:, t0:t0 + GROUP, :]
                hg = H[:, t0:t0 + GROUP, :]
                pool.wait_ge(s_got[g], 16 * GROUP * TOP * (run + 1))
                link.step(pool.tensor_scalar(hg, hg, 0.5, None, ALU.mult))
                for k in range(TOP):
                    for t in range(g * GROUP, (g + 1) * GROUP):
                        link.step(pool.tensor_scalar(Y[:, k, t, :], Y[:, k, t, :], share[:, half, k, t:t + 1], None,
                                                     ALU.mult))
                link.wait()
                link.step(pool.tensor_tensor(xg, xg, hg, ALU.add))
                link.wait()
                link.step(pool.tensor_tensor(xg, xg, Y[:, 0, g * GROUP:(g + 1) * GROUP, :], ALU.add))
                link.wait()
                pool.tensor_tensor(xg, xg, Y[:, 1, g * GROUP:(g + 1) * GROUP, :], ALU.add).then_inc(s_comb, 1)

            ones = const("ones")[:, 0:1].broadcast_to([P, E * INTER])
            pool.wait_ge(s_small, 16 * 6)
            for m in range(2):
                own = slice(m * E * INTER, (m + 1) * E * INTER)
                pool.wait_ge(s_gu_in[m], 16)
                pool.tensor_tensor(w_hi[:, m, :], swap[:, own], ones, ALU.mult).then_inc(s_hi, 1)
                pool.wait_ge(s_hi, m + 1)
                pool.tensor_tensor(w_lo[:, m, :], swap[:, own], w_hi[:, m, :].bitcast(F32), ALU.subtract
                                   ).then_inc(s_lo, 1)
            scatter(0)
            scatter(1)
            gather(0)
            pool.wait_ge(s_gu, TILES)
            pool.wait_ge(s_lo_out, 16 * 2)
            pool.memset(kz, 0.0).then_inc(s_kz, 1)
            pool.memset(vz, 0.0).then_inc(s_vz, 1)
            gather(1)
            for g in range(G):
                combine(1, g)
            scatter(2)
            scatter(3)
            gather(2)
            gather(3)

        @block.scalar
        def _(act):
            def fronts():
                for m0, m1, m2, m3, m4, m5 in front_steps():
                    if m3 is not None:
                        n2_rows(m3)
                    if m4 is not None:
                        n2_out(m4, bank[4 + m4 % 2])
                    if m0 is not None:
                        roots(m0)
                    if m1 is not None:
                        h_out(m1)
                        n1_out(m1, bank[m1 % 2])
                    if m2 is not None:
                        roots2(m2)
                    if m5 in (G - 1, 2 * G - 1):
                        top_exp(m5 // G)
                    if m5 == G - 1:
                        tables()

            def roots(m):
                act.wait_ge(s_var, m + 1)
                act.activation(root[:, m % 2], var2[:, m % 2], ACT.Sqrt).then_inc(s_root, 1)

            def n1_out(m, src, dst=n1T):
                act.wait_ge(s_n1p, m + 1)
                act.activation(dst[:, m % 2, :], src[:], ACT.Identity,
                               bias=col("ln1_b"), scale=col("ln1_g")).then_inc(s_n1T, 1)

            def h_out(m):
                act.wait_ge(s_n1, m + 1)
                t0 = RUNS[m // G][1] * T + m % G * GROUP
                for t in range(GROUP):
                    ins = act.activation(H[:, t0 + t, :], X[:, t0 + t, :], ACT.Identity,
                                         bias=shift[:, m % 2, t:t + 1], scale=rstd[:, m % 2, 0, t:t + 1])
                ins.then_inc(s_hn, 1)

            def n2_rows(m):
                layer, half = RUNS[m // G]
                s, t0 = m % G, half * T + m % G * GROUP
                if layer and s == 0:
                    act.wait_ge(s_scat[half], 16 * TOP * T * layer)
                    if half:
                        act.wait_ge(s_comb, 2 * G)
                act.wait_ge(s_rstd2, m + 1)
                for t in range(GROUP):
                    ins = act.activation(n2[half][:, s * GROUP + t, :], H[:, t0 + t, :], ACT.Identity,
                                         bias=shift2[:, m % 2, t:t + 1], scale=rstd2[:, m % 2, t:t + 1])
                ins.then_inc(s_n2, 1)

            def roots2(m):
                act.wait_ge(s_var2, m + 1)
                act.activation(root2[:, m % 2], mv2[:, m % 2, :, 1], ACT.Sqrt).then_inc(s_root2, 1)

            def n2_out(m, src):
                act.wait_ge(s_n2p, m + 1)
                act.activation(n2T[:, m % 2, :], src[:], ACT.Identity,
                               bias=col("ln2_b"), scale=col("ln2_g")).then_inc(s_n2T, 1)

            def top_exp(run):
                act.wait_ge(s_gap, run + 1)
                act.activation(wexp[:], gap2[:], ACT.Exp).then_inc(s_exp, 1)

            def last_front(part):
                m = group_no(LAST_FRONT)
                if part == "n1_out":
                    n1_out(m, bank[0])
                    h_out(m)
                if part == "roots2":
                    roots2(m)
                if part == "n2_rows":
                    n2_rows(m)
                if part == "n2_out":
                    n2_out(m, bank[0])
                if part == "top_exp":
                    top_exp(3)

            def experts(layer):
                base = layer * TILES

                def step(n, k):
                    k2 = (base + k) % 2
                    if not known(n) or n + 1 < TILES:
                        act.wait_ge(s_xp, n + (base + 2))
                        if not known(n) or base + n >= 1:
                            act.wait_ge(s_xlo, n + base)
                        act.activation(xsT[:, 1 - k2, :], bank[0][:, 0:P], ACT.Identity,
                                       bias=col("ln2_b"), scale=col("ln2_g"))
                        act.activation(x_hi[:, 1 - k2, :], bank[0][:, 0:P], ACT.Identity,
                                       bias=col("ln2_b"), scale=col("ln2_g")).then_inc(s_xT, 1)
                    if not known(n) or 0 <= n < TILES:
                        act.wait_ge(s_gu, n + (base + 1))
                        act.activation(sg[:, k2, :], bank[1 + k2][:], ACT.Silu).then_inc(s_sg, 1)
                    if not known(n) or 1 <= n < TILES + 1:
                        act.wait_ge(s_hp, n + base)
                        act.activation(hidT[:, 1 - k2, :], bank[5 + (1 - k2)][:], ACT.Copy).then_inc(s_hT, 1)
                    if layer == 0 and known(n) and n == ROOTS:
                        roots_of(0, 0, T)
                    if layer and known(n) and n in ACT_PARTS:
                        last_front(ACT_PARTS[n])

                steps(act, -1, ((LO[layer], HI),), TILES, UN, step)

            def decays():
                act.activation(expd_col[:], col("decay"), ACT.Exp)
                act.activation(expd_row[:], row("decay"), ACT.Exp).then_inc(s_tab, 1)

            def tables():
                act.wait_ge(s_tabv, 1)
                act.activation(w_chunk[:], negd_col[:], ACT.Exp, scale=float(P))
                act.activation(w_since[:], const("iota"), ACT.Exp, scale=negd_col[:])
                act.activation(w_until[:], negd_row[:], ACT.Exp, scale=const("left"))
                for h in range(HEADS):
                    ins = act.activation(wm[:, h, :], const("gap"), ACT.Exp, scale=negd_row[:, h * HD:h * HD + 1])
                ins.then_inc(s_tab, 1)

            def roots_of(k, t0, t1):
                act.wait_ge(s_avar, k + 1)
                act.activation(aroot[:, t0:t1], amv[:, t0:t1, 1], ACT.Sqrt).then_inc(s_aroot, 1)

            def attention():
                act.wait_ge(s_kz, 1)
                act.wait_ge(s_vz, 1)
                def step(n, p):
                    q = 1 - p
                    prep = not known(n) or n + 1 < NA
                    close = not known(n) or 1 <= n <= NA
                    front = group_no(FRONT[n]) if known(n) and n in FRONT else None
                    front_end = group_no(FRONT_END[n]) if known(n) and n in FRONT_END else None
                    if close:
                        act.wait_ge(s_cen, n)
                        if not known(n) or n >= 2:
                            act.wait_ge(s_z, n - 1)
                        act.activation(yc[:], bank[4][:, AT:2 * AT], ACT.Copy)
                        act.activation(sq[:], bank[4][:, AT:2 * AT], ACT.Square).then_inc(s_sq, 1)
                        act.wait_ge(s_yvar, n)
                        act.activation(yroot[:], bank[4][:, 0:AT], ACT.Sqrt, bias=const("eps")).then_inc(s_yroot, 1)
                    if front is not None and early(n):
                        roots(front)
                    if prep:
                        act.wait_ge(s_xnp, n + 2)
                        if known(n) and n == -1:
                            act.activation(xT[:, q, 0:1], consts[:, 0:1], ACT.Copy, scale=0.0)
                        else:
                            act.wait_ge(s_XT, n + 1)
                            act.activation(xT[:, q, 0:1], xT[:, p, AT:AT + 1], ACT.Copy,
                                           scale=0.0 if known(n) and n == NQ - 1 else 1.0)
                        act.activation(xT[:, q, 1:AT + 1], bank[6][:, 0:AT], ACT.Copy).then_inc(s_XT, 1)
                    if front_end is not None:
                        n2_rows(front_end)
                        n2_out(front_end, bank[5])
                    if front is not None and not early(n):
                        roots(front)
                    if front is not None:
                        h_out(front)
                    if known(n) and n in ROUTE:
                        top_exp(ROUTE[n])
                    if prep:
                        act.wait_ge(s_rkp, n + 2)
                        if not known(n) or n >= 0:
                            act.wait_ge(s_rx, n + 1)
                            act.wait_ge(s_rw, n + 1)
                        act.activation(rT, bank[7][:, 0:AT].rearrange("p (a t) -> p a t", a=AG), ACT.Copy)
                        for i in range(QUADS):
                            own = slice(32 * i, 32 * i + 32)
                            ins = act.activation(kz[own, q, i, :], bank[7][own, AT:2 * AT], ACT.Copy)
                        ins.then_inc(s_rk, 1)
                    if front is not None and early(n):
                        n1_out(front, bank[5], n2T)
                    if prep:
                        act.wait_ge(s_rk, n + 2)
                        for l in range(HQ):
                            ins = act.activation(rx[:, q, :, l, :], rT, ACT.Copy, scale=const("heads4")[:, l:l + 1])
                        ins.then_inc(s_rx, 1)
                        act.wait_ge(s_vgp, n + 2)
                        if close:
                            act.wait_ge(s_z, n)
                        for a in range(AG):
                            act.activation(v_own(q, a),
                                           bank[6][:, a * C:(a + 1) * C].rearrange("p (q l d) -> p q l d", l=HQ, d=HD),
                                           ACT.Copy)
                        act.activation(gT[:, q], bank[6][:, AT:2 * AT], ACT.Silu).then_inc(s_vg, 1)
                    if not known(n) or 0 <= n < NA:
                        act.wait_ge(s_av, n * 2 + 2)
                        act.activation(yT[:], bank[4][:, 0:AT], ACT.Copy, scale=1.0 / HD).then_inc(s_y8, 1)
                    if known(n) and n == NA - 1:
                        act.wait_ge(s_lo_out, 16 * 2)
                        act.dma_start(swap[:, E * INTER:], lo_store[1]).then_inc(s_lo_in[1], 16)
                    if front is not None and not early(n):
                        n1_out(front, bank[5], n2T)
                    if front is not None:
                        roots2(front)
                    if known(n) and n in STATS:
                        g = STATS[n]
                        roots_of(1 + g, T + g * GROUP, T + (g + 1) * GROUP)

                attention_steps(act, step)

            act.wait_ge(s_small, 16 * 6)
            decays()
            fronts()
            experts(0)
            attention()
            roots(group_no(LAST_FRONT))
            experts(1)

        def stored(n, k, base):
            rest = (base + k - 2) % 4
            if known(n):
                return 16 * ((base + n - 2) // 4)
            return n * 4 + (4 * (base - 2 - rest))

        @block.vector
        def _(dve):
            link = Chain(dve, s_dve)

            def norm_stats(run, s):
                n = run * G + s
                par = n % 2
                t0 = RUNS[run][1] * T + s * GROUP
                if run == 0 or run == 1:
                    dve.wait_ge(s_x[run * G + s], 16)
                link.wait()
                for t in range(GROUP):
                    link.step(dve.bn_stats(bn[:, t, :], X[:, t0 + t, :]))
                link.wait()
                for t in range(GROUP):
                    link.step(dve.bn_aggr(mv[:, par, t, :], bn[:, t, :]))
                link.wait()
                link.step(dve.tensor_scalar(var2[:, par, 0, :], mv[:, par, :, 1], EPS, None, ALU.add))
                dve.tensor_scalar(var2[:, par, 1, :], mv[:, par, :, 1], 1.0 + EPS, EPS * EPS,
                                  ALU.mult, ALU.add).then_inc(s_var, 1)
                link.wait()

            def norm_apply(run, s):
                n = run * G + s
                par = n % 2
                t0 = RUNS[run][1] * T + s * GROUP
                dve.wait_ge(s_root, n + 1)
                if n >= 2:
                    dve.wait_ge(s_hn, n - 1)
                link.step(dve.reciprocal(rstd[:, par], root[:, par]))
                link.wait()
                dve.scalar_tensor_tensor(shift[:, par], mv[:, par, :, 0], -1.0, rstd[:, par, 0, :],
                                         ALU.mult, ALU.mult)
                if n >= 2:
                    dve.wait_ge(s_n1p, n - 1)
                for t in range(GROUP):
                    ins = dve.tensor_scalar(n1[:, par, t, :], X[:, t0 + t, :], mv[:, par, t, 0:1],
                                            rstd[:, par, 1, t:t + 1], ALU.subtract, ALU.mult)
                ins.then_inc(s_n1, 1)

            def add_proj(run, s, src=None):
                n = run * G + s
                par = n % 2
                t0 = RUNS[run][1] * T + s * GROUP
                dve.wait_ge(s_proj, n + 1)
                dve.wait_ge(s_hn, n + 1)
                link.wait()
                hg = H[:, t0:t0 + GROUP, :]
                src = src or bank[2 + par]
                dve.tensor_tensor(hg, hg, src[:].rearrange("p (t c) -> p t c", c=C), ALU.add).then_inc(s_h, 1)
                dve.wait_ge(s_h, n + 1)
                for t in range(GROUP):
                    link.step(dve.bn_stats(bn[:, t, :], H[:, t0 + t, :]))
                link.wait()
                for t in range(GROUP):
                    link.step(dve.bn_aggr(mv2[:, par, t, :], bn[:, t, :]))
                link.wait()
                dve.tensor_scalar(mv2[:, par, :, 1], mv2[:, par, :, 1], EPS, None, ALU.add).then_inc(s_var2, 1)

            def norm2_scale(run, s):
                n = run * G + s
                par = n % 2
                dve.wait_ge(s_root2, n + 1)
                if n >= 2:
                    dve.wait_ge(s_n2, n - 1)
                link.step(dve.reciprocal(rstd2[:, par], root2[:, par]))
                link.wait()
                dve.scalar_tensor_tensor(shift2[:, par], mv2[:, par, :, 0], -1.0, rstd2[:, par],
                                         ALU.mult, ALU.mult).then_inc(s_rstd2, 1)

            def logits(run, s, src=bank[6]):
                n = run * G + s
                dve.wait_ge(s_logit, n + 1)
                dve.tensor_copy(L[:, s * GROUP:(s + 1) * GROUP, :],
                                src[:, 0:GROUP * E].rearrange("p (t e) -> p t e", e=E)).then_inc(s_logc, 1)

            def per_tile(v):
                return v.unsqueeze(2).broadcast_to([P, T, E])

            def per_expert(v, n=T):
                return v.unsqueeze(1).broadcast_to([P, n, E])

            def route(run):
                route_picks(run)
                route_counts(run, bank[7])
                route_slots(run)

            def route_picks(run):
                layer, half = RUNS[run]
                rank = per_expert(const("rank"))
                dve.wait_ge(s_logc, (run + 1) * G)
                src = L
                for k in range(TOP):
                    link.step(dve.tensor_reduce(best[:, k], src[:], AX, ALU.max))
                    link.wait()
                    link.step(dve.tensor_tensor(eq[:], src[:], per_tile(best[:, k]), ALU.is_equal))
                    link.wait()
                    link.step(dve.tensor_tensor(eq[:], eq[:], rank, ALU.mult))
                    link.wait()
                    link.step(dve.tensor_reduce(first[:], eq[:], AX, ALU.max))
                    link.wait()
                    link.step(dve.tensor_tensor(pick[:, k], rank, per_tile(first[:]), ALU.is_equal))
                    link.wait()
                    if k == 0:
                        link.step(dve.scalar_tensor_tensor(L2[:], pick[:, 0], -BIG, L[:], ALU.mult, ALU.add))
                        link.wait()
                        src = L2
                dve.tensor_tensor(gap2[:], best[:, 1], best[:, 0], ALU.subtract).then_inc(s_gap, 1)
                dve.tensor_tensor(both[:], pick[:, 0], pick[:, 1], ALU.add).then_inc(s_pick, 1)

            def route_counts(run, src):
                dve.wait_ge(s_count, run + 1)
                link.wait()
                dve.tensor_copy(counts[:], src[:, T * E:2 * T * E].rearrange("p (t e) -> p e t", e=E))
                dve.tensor_copy(ahead[:], src[:, 0:T * E].rearrange("p (t e) -> p t e", e=E)).then_inc(s_cntc, 1)

            def route_slots(run):
                layer, half = RUNS[run]
                dve.wait_ge(s_exp, run + 1)
                link.step(dve.tensor_scalar(wden[:], wexp[:], 1.0, 2.0, ALU.add, ALU.mult))
                link.wait()
                link.step(dve.reciprocal(share[:, half, 0], wden[:]))
                link.wait()
                link.step(dve.tensor_tensor(share[:, half, 1], share[:, half, 0], wexp[:], ALU.mult))
                dve.wait_ge(s_cntc, run + 1)
                ones = ones_et[:].rearrange("p e t -> p (e t)")
                link.step(dve.tensor_tensor_scan(cum[:].rearrange("p e t -> p (e t)"), ones,
                                                 counts[:].rearrange("p e t -> p (e t)"), 0.0, ALU.mult, ALU.add))
                link.wait()
                link.step(dve.tensor_tensor(over[:], cum[:, :, T - 1:T].broadcast_to([P, E, T]),
                                            const("limit").unsqueeze(1).broadcast_to([P, E, T]), ALU.is_gt))
                link.wait()
                link.step(dve.tensor_reduce(tiles_e[:], over[:], AX, ALU.add))
                link.wait()
                link.step(dve.tensor_tensor_scan(ends[:], const("ones")[:, 0:E], tiles_e[:], 0.0, ALU.mult, ALU.add))
                link.wait()
                link.step(dve.tensor_tensor(start[:], ends[:], tiles_e[:], ALU.subtract))
                link.wait()
                link.step(dve.tensor_tensor(cum[:], cum[:], counts[:], ALU.subtract))
                link.wait()
                link.step(dve.tensor_tensor(slot_e[:], cum[:].rearrange("p e t -> p t e"), ahead[:], ALU.add))
                link.wait()
                link.step(dve.scalar_tensor_tensor(slot_e[:], per_expert(start[:]), float(P), slot_e[:],
                                                   ALU.mult, ALU.add))
                for k in range(TOP):
                    link.wait()
                    link.step(dve.tensor_tensor(eq[:], slot_e[:], pick[:, k], ALU.mult))
                    link.wait()
                    link.step(dve.tensor_reduce(slot_f[:, k], eq[:], AX, ALU.add))
                n = XT
                link.step(dve.tensor_tensor(done_e[:], per_expert(ends[:], n),
                                            const("tile").unsqueeze(2).broadcast_to([P, n, E]), ALU.is_le))
                link.wait()
                link.step(dve.tensor_reduce(tile_ef[:], done_e[:], AX, ALU.add))
                link.wait()
                link.step(dve.tensor_scalar(tile_e[:, half * XT:(half + 1) * XT], tile_ef[:], float(E - 1), float(INTER),
                                            ALU.min, ALU.mult))
                link.wait()
                dve.tensor_copy(slot[:, half], slot_f[:]).then_inc(s_table, 1)

            def fronts():
                for m0, m1, m2, m3, m4, m5 in front_steps():
                    if m3 is not None:
                        norm2_scale(m3 // G, m3 % G)
                    if m0 is not None:
                        norm_stats(m0 // G, m0 % G)
                    if m1 is not None:
                        norm_apply(m1 // G, m1 % G)
                    if m2 is not None:
                        add_proj(m2 // G, m2 % G)
                    if m5 is not None:
                        logits(m5 // G, m5 % G)
                    if m5 in (G - 1, 2 * G - 1):
                        route(m5 // G)

            def last_front(part):
                if part == "add_proj":
                    add_proj(*LAST_FRONT, bank[0])
                if part == "scale":
                    norm2_scale(*LAST_FRONT)
                if part == "logits":
                    logits(*LAST_FRONT, bank[0])
                if part == "picks":
                    route_picks(3)
                if part == "counts":
                    route_counts(3, bank[0])
                if part == "slots":
                    route_slots(3)

            def experts(layer):
                base = layer * TILES

                def step(n, k):
                    k2 = (base + k) % 2
                    if not known(n) or n + 1 < TILES:
                        dve.wait_ge(s_xT, n + (base + 2))
                        dve.tensor_tensor(x_lo[:, 1 - k2, :], xsT[:, 1 - k2, :], x_hi[:, 1 - k2, :].bitcast(F32),
                                          ALU.subtract).then_inc(s_xlo, 1)
                    if not known(n) or 0 <= n < TILES:
                        dve.wait_ge(s_sg, n + (base + 1))
                        dve.tensor_tensor(hid[:, k2, :], sg[:, k2, :], bank[3 + k2][:],
                                          ALU.mult).then_inc(s_hid, 1)
                    if not known(n) or n >= 2:
                        j = (base + k - 2) % 4
                        dve.wait_ge(s_y, n + (base - 1))
                        if not known(n) or base + n - 2 >= 4:
                            dve.wait_ge(s_store[j], stored(n, k, base))
                        dve.tensor_copy(ys[:, j, :], bank[7][:, 0:C]).then_inc(s_yc, 1)
                    if layer and known(n) and n in DVE_PARTS:
                        last_front(DVE_PARTS[n])
                    if known(n) and COMBINED <= n < COMBINED + 2 * G:
                        g = (n - COMBINED) // 2
                        if (n - COMBINED) % 2 == 0:
                            combine(2 * layer, g)
                        elif layer == 0:
                            dve.wait_ge(s_comb, g + 1)
                            combined_stats(0, g)
                    if layer == 0 and known(n) and 0 <= n < 3:
                        decay_table(n)
                    if layer == 0 and known(n) and n == ROOTS - 1:
                        attn_variances(0, T)
                    if layer == 0 and known(n) and n == ROOTS + 2:
                        attn_rstd(0, 0, T)
                        normalize(-1)

                steps(dve, -1, ((LO[layer], COMBINED),), TILES + 1, UN, step)

            def add_h(run, g):
                t0 = RUNS[run][1] * T + g * GROUP
                xg = X[:, t0:t0 + GROUP, :]
                link.wait()
                link.step(dve.scalar_tensor_tensor(xg, H[:, t0:t0 + GROUP, :], 0.5, xg, ALU.mult, ALU.add))

            def combine(run, g):
                layer, half = RUNS[run]
                t0 = half * T + g * GROUP
                dve.wait_ge(s_got[g], 16 * GROUP * TOP * (run + 1))
                if run != 3:
                    add_h(run, g)
                link.wait()
                for k in range(TOP):
                    for t in range(GROUP):
                        ins = dve.scalar_tensor_tensor(
                            X[:, t0 + t, :], Y[:, k, g * GROUP + t, :], share[:, half, k, g * GROUP + t:g * GROUP + t + 1],
                            X[:, t0 + t, :], ALU.mult, ALU.add)
                        if k == 0:
                            link.step(ins)
                    if k == 0:
                        link.wait()
                ins.then_inc(s_comb, 1)

            def combined_stats(run, g):
                half = RUNS[run][1]
                dve.wait_ge(s_comb, run * G + g + 1)
                link.wait()
                for t in range(g * GROUP, (g + 1) * GROUP):
                    link.step(dve.bn_stats(abn[:, t, :], X[:, half * T + t, :]))
                link.wait()
                for t in range(g * GROUP, (g + 1) * GROUP):
                    link.step(dve.bn_aggr(amv[:, half * T + t, :], abn[:, t, :]))

            def decays():
                dve.wait_ge(s_tab, 1)
                dve.tensor_scalar(negd_col[:], expd_col[:], DECAY_MAX, -1.0, ALU.min, ALU.mult)
                dve.tensor_scalar(negd_row[:], expd_row[:], DECAY_MAX, -1.0, ALU.min, ALU.mult).then_inc(s_tabv, 1)

            def decay_table(k):
                if k == 0:
                    dve.wait_ge(s_tab, 2)
                    link.step(dve.tensor_tensor(wm[:], wm[:], const("later").unsqueeze(1).broadcast_to([P, HEADS, P]),
                                                ALU.mult))
                    return
                link.wait()
                for h in range((k - 1) * HEADS // 2, k * HEADS // 2):
                    link.step(dve.scalar_tensor_tensor(wm[:, h, :], ident, bonus[:, h:h + 1], wm[:, h, :],
                                                       ALU.mult, ALU.add))

            def attn_variances(t0, t1):
                link.wait()
                dve.tensor_scalar(amv[:, t0:t1, 1], amv[:, t0:t1, 1], EPS, None, ALU.add).then_inc(s_avar, 1)

            def normalize(n):
                if not known(n) or n >= 0:
                    dve.wait_ge(s_xnp, n + 1)
                for a in range(AG):
                    tile = bass.ds(n * AG + (AG + a), 1)
                    ins = dve.tensor_scalar(xn[:, a, :], X[:, tile, :], amv[:, tile, 0], arstd[:, tile],
                                            ALU.subtract, ALU.mult)
                ins.then_inc(s_xn, 1)

            def attn_rstd(k, t0, t1):
                dve.wait_ge(s_aroot, k + 1)
                link.step(dve.reciprocal(arstd[:, t0:t1], aroot[:, t0:t1]))
                link.wait()

            def attention():
                link.step(dve.memset(state[:, 0, :], 0.0))
                for k in range(4):
                    dve.wait_ge(s_store[k], 16 * len([n for n in range(TILES) if n % 4 == k]))

                def mask(n, c):
                    if not known(n) or n >= 1:
                        dve.wait_ge(s_av, n * 2 + (c - 1))
                    for q in range(4):
                        dve.wait_ge(s_sc, n * 8 + (4 * c + q + 1))
                        dve.tensor_tensor(att[:, c, 4 * q:4 * q + 4, :],
                                          bank[q][:].rearrange("p (h i) -> p h i", i=P),
                                          wm[:, 4 * q:4 * q + 4, :], ALU.mult).then_inc(s_att, 1)

                def group_norm(n, q):
                    dve.wait_ge(s_yroot, n)
                    dve.reciprocal(yroot[:], yroot[:]).then_inc(s_yrstd, 1)
                    dve.wait_ge(s_yrstd, n)
                    dve.scalar_tensor_tensor(yn[:], yc[:], col("ln_w"), yroot[:], ALU.mult, ALU.mult).then_inc(s_yn, 1)
                    dve.wait_ge(s_yn, n)
                    dve.wait_ge(s_vg, n)
                    if not known(n) or n >= 2:
                        dve.wait_ge(s_o, n - 1)
                    dve.scalar_tensor_tensor(zT[:], yn[:], col("ln_b"), gT[:, q], ALU.add, ALU.mult).then_inc(s_z, 1)

                def kv_blocks(n):
                    dve.wait_ge(s_kv, n + 1)
                    if not known(n) or n >= 1:
                        dve.wait_ge(s_state, n * 2)
                    dve.tensor_tensor(add[:], bank[6][:, 0:AT].rearrange("p (a c) -> p a c", a=AG),
                                      const("block").unsqueeze(1).broadcast_to([P, AG, C]), ALU.mult
                                      ).then_inc(s_add, 1)
                    dve.wait_ge(s_add, n + 1)

                def update(n, c):
                    if c == 1:
                        dve.wait_ge(s_state, n * 2 + 1)
                    if c == 1 or not known(n) or n >= 1:
                        dve.wait_ge(s_av, n * 2 + c)
                    if known(n) and n == NQ - 1 and c == 1:
                        dve.memset(state[:, 0, :], 0.0).then_inc(s_state, 1)
                    else:
                        dve.scalar_tensor_tensor(state[:, 1 - c, :], state[:, c, :], w_chunk[:], add[:, c, :],
                                                 ALU.mult, ALU.add).then_inc(s_state, 1)

                def step(n, p):
                    prep = not known(n) or n + 1 < NA
                    core = not known(n) or 0 <= n < NA
                    close = not known(n) or 1 <= n <= NA
                    front = FRONT.get(n) if known(n) else None
                    front_end = FRONT_END.get(n) if known(n) else None
                    run = ROUTE.get(n) if known(n) else None
                    q = 1 - p
                    if known(n) and n - 1 in STATS:
                        g = STATS[n - 1]
                        attn_rstd(1 + g, T + g * GROUP, T + (g + 1) * GROUP)
                    if not known(n) or 0 <= n and prep:
                        normalize(n)
                    if front and early(n):
                        stats(n, *front)
                    if front_end:
                        norm2_scale(*front_end)
                    if core:
                        mask(n, 0)
                    if front and early(n):
                        norm_apply(*front)
                    if prep:
                        dve.wait_ge(s_XT, n + 2)
                        dve.tensor_tensor(delta, xT[:, q, 1:AT + 1], xT[:, q, 0:AT], ALU.subtract).then_inc(s_delta, 1)
                        dve.wait_ge(s_delta, n + 2)
                        if not known(n) or n >= 0:
                            dve.wait_ge(s_kp, n + 1)
                        for i, m in enumerate("rkvg"):
                            ins = dve.scalar_tensor_tensor(mix[:, i, :], delta, col("mix_" + m), xT[:, q, 0:AT],
                                                           ALU.mult, ALU.add)
                        ins.then_inc(s_mix, 1)
                    if not known(n) or 2 <= n < NA + 2:
                        dve.wait_ge(s_o, n - 1)
                        t0 = n * AG + (-2 * AG)
                        xg = X[:, bass.ds(t0, AG), :]
                        dve.tensor_tensor(xg, xg, bank[7][:, 0:AT].rearrange("p (a c) -> p a c", a=AG),
                                          ALU.add).then_inc(s_xa, 1)
                    if core:
                        kv_blocks(n)
                        update(n, 0)
                    if close:
                        group_norm(n, q)
                    if front_end:
                        logits(*front_end, bank[5])
                    if run is not None:
                        route_picks(run)
                    if front and not early(n):
                        stats(n, *front)
                    if core:
                        mask(n, 1)
                    if front and not early(n):
                        norm_apply(*front)
                    if run is not None:
                        route_counts(run, bank[5])
                    if prep:
                        dve.wait_ge(s_rk, n + 2)
                        dve.tensor_tensor(rw[:, q], rT, w_since[:].unsqueeze(1).broadcast_to([P, AG, P]),
                                          ALU.mult).then_inc(s_rw, 1)
                        dve.wait_ge(s_kp, n + 2)
                        dve.tensor_tensor(kw[:, q], bank[7][:, 0:AT].rearrange("p (a c) -> p a c", a=AG),
                                          w_until[:].unsqueeze(1).broadcast_to([P, AG, C]), ALU.mult).then_inc(s_kw, 1)
                    if core:
                        update(n, 1)
                    if front:
                        add_proj(*front, bank[5])
                    if run is not None:
                        route_slots(run)
                    if known(n) and n in STATS:
                        g = STATS[n]
                        combined_stats(1, g)
                        attn_variances(T + g * GROUP, T + (g + 1) * GROUP)

                def stats(n, run, g):
                    dve.wait_ge(s_xa, rows_ready(run, g))
                    norm_stats(run, g)

                attention_steps(dve, step)

            link.step(dve.memset(ones_et[:], 1.0))
            link.wait()
            link.step(dve.memset(ones_et[:, :, 0:1], 0.0))
            dve.wait_ge(s_small, 16 * 6)
            decays()
            fronts()
            experts(0)
            attention()
            dve.wait_ge(s_xa, rows_ready(*LAST_FRONT))
            norm_stats(*LAST_FRONT)
            norm_apply(*LAST_FRONT)
            experts(1)
            for g in range(G):
                add_h(3, g)
            for g in range(G):
                combine(3, g)

        @block.tensor
        def _(pe):
            def fronts():
                for m0, m1, m2, m3, m4, m5 in front_steps():
                    if m2 is not None:
                        if m2 >= 2:
                            pe.wait_ge(s_h, m2 - 1)
                        project(m2, bank[2 + m2 % 2])
                    if m4 is not None:
                        if m4 >= 2:
                            pe.wait_ge(s_n2T, m4 - 1)
                        n2_turn(m4, bank[4 + m4 % 2])
                    if m5 is not None:
                        if m5 >= 1:
                            pe.wait_ge(s_logc, m5)
                        gate_logits(m5, bank[6])
                    if m1 is not None:
                        if m1 >= 2:
                            pe.wait_ge(s_n1T, m1 - 1)
                        n1_turn(m1, bank[m1 % 2])
                    if m5 in (G - 1, 2 * G - 1):
                        run = m5 // G
                        if run:
                            pe.wait_ge(s_cntc, run)
                        count(run, bank[7])

            def n1_turn(m, dst):
                pe.wait_ge(s_n1, m + 1)
                for t in range(GROUP):
                    mm = pe.transpose(dst[:, t * P:(t + 1) * P], n1[:, m % 2, t, :], ident)
                mm.then_inc(s_n1p, 1)

            def project(m, dst, src=n1T):
                pe.wait_ge(s_n1T, m + 1)
                for t in range(GROUP):
                    mm = pe.matmul(dst[:, t * C:(t + 1) * C], src[:, m % 2, t * P:(t + 1) * P],
                                   weight("proj"), start=True, stop=True)
                mm.then_inc(s_proj, 1)

            def n2_turn(m, dst):
                pe.wait_ge(s_n2, m + 1)
                half, s = RUNS[m // G][1], m % G
                for t in range(GROUP):
                    mm = pe.transpose(dst[:, t * P:(t + 1) * P], n2[half][:, s * GROUP + t, :], ident)
                mm.then_inc(s_n2p, 1)

            def gate_logits(m, dst):
                pe.wait_ge(s_n2T, m + 1)
                for t in range(GROUP):
                    mm = pe.matmul(dst[:, t * E:(t + 1) * E], n2T[:, m % 2, t * P:(t + 1) * P],
                                   gate[:], start=True, stop=True)
                mm.then_inc(s_logit, 1)

            def count(run, dst):
                pe.wait_ge(s_pick, run + 1)
                flat = both[:].rearrange("p t e -> p (t e)")
                pe.matmul(dst[:, 0:T * E], const("before"), flat, start=True, stop=True)
                pe.matmul(dst[:, T * E:2 * T * E], const("ones"), flat, start=True, stop=True
                          ).then_inc(s_count, 1)

            def last_front(part):
                m = group_no(LAST_FRONT)
                if part == "n1_turn":
                    n1_turn(m, bank[0])
                if part == "project":
                    project(m, bank[0])
                if part == "n2_turn":
                    n2_turn(m, bank[0])
                if part == "logits":
                    gate_logits(m, bank[0])
                if part == "count":
                    count(3, bank[0])

            def last_front_read(part):
                m = group_no(LAST_FRONT)
                if part == "n1_turn":
                    pe.wait_ge(s_n1T, m + 1)
                if part == "project":
                    pe.wait_ge(s_h, m + 1)
                if part == "n2_turn":
                    pe.wait_ge(s_n2T, m + 1)
                if part == "logits":
                    pe.wait_ge(s_logc, m + 1)
                if part == "count":
                    pe.wait_ge(s_cntc, 4)

            def experts(layer):
                base = layer * TILES

                def expert_of(n):
                    return pe.value_load(tile_e[0:1, bass.ds(n, 1)], min_val=0, max_val=(E - 1) * INTER)

                def step(n, k):
                    k2 = (base + k) % 2
                    k4 = (base + k + 1) % 4
                    if known(n) and n in (0, XT):
                        pe.wait_ge(s_table, layer * HALVES + n // XT + 1)
                    if known(n) and n == 0:
                        for m in range(2):
                            if layer:
                                pe.wait_ge(s_lo_in[m], 16)
                            else:
                                pe.wait_ge(s_lo, m + 1)
                        pe.wait_ge(s_down_in, 16)
                    if not known(n) or n + 1 < TILES:
                        if known(n):
                            pe.wait_ge(s_load[k4], 16 * ((base + n + 1) // 4 + 1))
                        else:
                            pe.wait_ge(s_load[k4], n * 4 + (4 * (base + 1 - k4) + 16))
                        if not known(n) or n >= 0:
                            pe.wait_ge(s_xlo, n + (base + 1))
                        elif layer:
                            pe.wait_ge(s_xT, base)
                        if layer and known(n) and n - 1 in PE_PARTS:
                            last_front_read(PE_PARTS[n - 1])
                        pe.transpose(bank[0][:, 0:P], xs[:, k4, :], ident).then_inc(s_xp, 1)
                    if not known(n) or 0 <= n < TILES:
                        at = expert_of(n)
                        if known(n) and n + 1 == TILES:
                            pe.wait_ge(s_xlo, n + (base + 1))
                        for x, w in ((x_hi, w_hi), (x_hi, w_lo), (x_lo, w_hi)):
                            for m in range(2):
                                mm = pe.matmul(bank[1 + 2 * m + k2][:], x[:, k2, :], w[:, m, bass.ds(at, INTER)],
                                               start=w is w_hi and x is x_hi, stop=x is x_lo,
                                               skip_group_check=True)
                        mm.then_inc(s_gu, 1)
                    if not known(n) or 1 <= n < TILES + 1:
                        pe.wait_ge(s_hid, n + base)
                        for c in range(CH):
                            mm = pe.transpose(bank[5 + (1 - k2)][:, c * P:(c + 1) * P],
                                              hid[:, 1 - k2, c * P:(c + 1) * P], ident)
                        mm.then_inc(s_hp, 1)
                    if not known(n) or 2 <= n < TILES + 2:
                        at = expert_of(n - 2)
                        pe.wait_ge(s_hT, n + (base - 1))
                        if not known(n) or base + n - 2 >= 1:
                            pe.wait_ge(s_yc, n + (base - 2))
                        for c in range(CH):
                            mm = pe.matmul(bank[7][:, 0:C], hidT[:, k2, c * P:(c + 1) * P],
                                           wd[:, bass.ds(at + c * P, C)], start=(c == 0), stop=(c == CH - 1))
                        mm.then_inc(s_y, 1)
                    if layer and known(n) and n in PE_PARTS:
                        pe.wait_ge(s_xT, n + (base + 2))
                        last_front(PE_PARTS[n])

                steps(pe, -1, ((LO[layer], MID[0]), (MID[1], HI)), TILES + 1, UN, step)

            def attention():
                pe.wait_ge(s_yc, TILES)

                def scores(n, p, c, quads):
                    for q in quads:
                        if not known(n) or c or n >= 1:
                            pe.wait_ge(s_att, n * 8 + (4 * c + q - 3))
                        pe.matmul(bank[q][:], kz[:, p, q, c * P:(c + 1) * P],
                                  rx[:, p, c].rearrange("p l i -> p (l i)"),
                                  start=True, stop=True).then_inc(s_sc, 1)

                def kv(n, p):
                    pe.wait_ge(s_kw, n + 1)
                    pe.wait_ge(s_vg, n + 1)
                    if not known(n) or n + 1 < NA:
                        pe.wait_ge(s_XT, n + 2)
                    for c in range(AG):
                        mm = pe.matmul(bank[6][:, c * C:(c + 1) * C], kw[:, p, c, :], v_own(p, c),
                                       start=True, stop=True)
                    mm.then_inc(s_kv, 1)

                def front_n1(front):
                    pe.wait_ge(s_logc, front)
                    pe.wait_ge(s_cntc, front // G)
                    n1_turn(front, bank[5])

                def chunk_out(n, p, c):
                    if c == 0 and (not known(n) or n >= 1):
                        pe.wait_ge(s_y8, n)
                        pe.wait_ge(s_yroot, n)
                    if not known(n) or c or n >= 1:
                        pe.wait_ge(s_state, n * 2 + c)
                    pe.matmul(bank[4][:, c * P:(c + 1) * P], state[:, c, :], rw[:, p, c, :], start=True, stop=False,
                              skip_group_check=True)
                    pe.wait_ge(s_att, n * 8 + (4 * c + 4))
                    for l in range(HQ):
                        for q in range(QUADS):
                            mm = pe.matmul(bank[4][32 * q:32 * q + 32, c * P:(c + 1) * P],
                                           vz[:, p, c, q, 32 * l:32 * l + 32], att[:, c, q * HQ + l, :],
                                           start=False, stop=(l == HQ - 1), skip_group_check=True)
                    mm.then_inc(s_av, 1)

                def step(n, p):
                    prep = not known(n) or n + 1 < NA
                    core = not known(n) or 0 <= n < NA
                    close = not known(n) or 1 <= n <= NA
                    front = group_no(FRONT[n]) if known(n) and n in FRONT else None
                    front_end = group_no(FRONT_END[n]) if known(n) and n in FRONT_END else None
                    q = 1 - p
                    if core:
                        pe.wait_ge(s_rx, n + 1)
                        pe.wait_ge(s_rw, n + 1)
                        scores(n, p, 0, (0, 1))
                    if close:
                        pe.wait_ge(s_y8, n)
                        pe.matmul(bank[4][:, AT:2 * AT], const("centre"), yT[:], start=True, stop=True
                                  ).then_inc(s_cen, 1)
                    if core:
                        scores(n, p, 0, (2, 3))
                    if close:
                        pe.wait_ge(s_sq, n)
                        pe.matmul(bank[4][:, 0:AT], const("average"), sq[:], start=True, stop=True
                                  ).then_inc(s_yvar, 1)
                    if prep:
                        pe.wait_ge(s_xn, n + 2)
                        if not known(n) or n >= 0:
                            pe.wait_ge(s_vg, n + 1)
                        for a in range(AG):
                            mm = pe.transpose(bank[6][:, a * P:(a + 1) * P], xn[:, a, :], ident)
                        mm.then_inc(s_xnp, 1)
                    if not known(n) or 2 <= n < NA + 2:
                        pe.wait_ge(s_z, n - 1)
                        if not known(n) or n < NA:
                            pe.wait_ge(s_kw, n + 1)
                        elif n > NA:
                            pe.wait_ge(s_xa, n - 2)
                        for a in range(AG):
                            mm = pe.matmul(bank[7][:, a * C:(a + 1) * C], zT[:, a * P:(a + 1) * P], weight("o"),
                                           start=True, stop=True)
                        mm.then_inc(s_o, 1)
                    if core:
                        chunk_out(n, p, 0)
                    if front_end is not None:
                        pe.wait_ge(s_h, front_end + 1)
                        n2_turn(front_end, bank[5])
                    if core:
                        kv(n, p)
                        scores(n, p, 1, (0, 1))
                    if front_end is not None:
                        gate_logits(front_end, bank[5])
                    if prep:
                        pe.wait_ge(s_mix, n + 2)
                        if not known(n) or n >= 2:
                            pe.wait_ge(s_xa, n - 1)
                        elif n >= 0:
                            pe.wait_ge(s_kw, n + 1)
                        for i, m in enumerate("rk"):
                            mm = pe.matmul(bank[7][:, i * AT:(i + 1) * AT], weight(m), mix[:, i, :],
                                           start=True, stop=True)
                        mm.then_inc(s_rkp, 1)
                    if core:
                        scores(n, p, 1, (2, 3))
                    if front is not None and early(n):
                        front_n1(front)
                    if prep:
                        pe.wait_ge(s_XT, n + 2)
                        if core:
                            pe.wait_ge(s_add, n + 1)
                        for a in range(AG):
                            pe.matmul(bank[6][:, a * C:(a + 1) * C], mix[:, 2, a * P:(a + 1) * P], weight("v"),
                                      start=True, stop=True)
                        mm = pe.matmul(bank[6][:, AT:2 * AT], weight("g"), mix[:, 3, :], start=True, stop=True)
                        mm.then_inc(s_vgp, 1)
                        pe.wait_ge(s_rk, n + 2)
                        for a in range(AG):
                            mm = pe.matmul(bank[7][:, a * C:(a + 1) * C], mix[:, 1, a * P:(a + 1) * P], weight("k"),
                                           start=True, stop=True)
                        mm.then_inc(s_kp, 1)
                    if known(n) and n in ROUTE:
                        pe.wait_ge(s_logc, (ROUTE[n] + 1) * G)
                        count(ROUTE[n], bank[5])
                    if front is not None and early(n):
                        project(front, bank[5], n2T)
                    if core:
                        chunk_out(n, p, 1)
                    if front is not None and not early(n):
                        front_n1(front)
                        project(front, bank[5], n2T)

                attention_steps(pe, step)

            pe.wait_ge(s_small, 16 * 6)
            fronts()
            experts(0)
            attention()
            experts(1)


def _constants():
    import numpy as np
    c = np.zeros((P, NCONST), np.float32)
    p = np.arange(P)

    def put(name, v):
        a, b = CONST[name]
        c[:, a:b] = v
    put("ident", np.eye(P))
    put("before", p[:, None] < p[None, :])
    put("ones", 1.0)
    put("later", p[None, :] > p[:, None])
    put("gap", np.maximum(p[None, :] - p[:, None] - 1, 0))
    put("iota", p[None, :])
    put("block", p[:, None] // HD == p[None, :] // HD)
    put("centre", np.eye(P) - (p[:, None] // HD == p[None, :] // HD) / HD)
    put("average", (p[:, None] // HD == p[None, :] // HD) / HD)
    put("eps", EPS)
    put("heads4", (p[:, None] // HD) % HQ == np.arange(HQ)[None, :])
    put("left", (P - 1 - p)[:, None])
    put("rank", (E - np.arange(E))[None, :])
    put("limit", (P * np.arange(T))[None, :])
    put("tile", np.arange(XT)[None, :])
    return c


def kernel(**inputs):
    import numpy as _np
    import concourse.bacc as _bacc
    from concourse import mybir as _mybir
    from concourse.bass_utils import run_bass_kernel_spmd as _run

    def get(name):
        return _np.asarray(inputs["L0_" + name])

    ffn, attn = "ffn_", "attn_"
    decay = _np.repeat(get("attn_time_decay"), HD)
    arrays = {
        "x": get("attn_xq").reshape(HALVES * SEQ, C),
        "consts": _constants(),
        "cols": _np.stack([get("ffn_ln1_g"), get("ffn_ln1_b"), get("ffn_ln2_g"), get("ffn_ln2_b")]
                          + [get("attn_time_mix_" + m).reshape(C) for m in "rkvg"]
                          + [decay, get("attn_ln_w"), get("attn_ln_b")], axis=1),
        "rows": _np.stack([_np.broadcast_to(decay[None, :], (P, C))], axis=1),
        "bonus": _np.broadcast_to(get("attn_time_faaaa")[None, :], (P, HEADS)),
        "weights": _np.stack([get("ffn_attn_w").T] + [get("attn_W_" + m).T for m in "rkvgo"], axis=1),
        "gate": get("ffn_gate_w").T,
        "wg": get("ffn_gate_proj").transpose(2, 0, 1).reshape(C, E * INTER),
        "wu": get("ffn_up_proj").transpose(2, 0, 1).reshape(C, E * INTER),
        "wd": get("ffn_down_proj").reshape(E, C, CH, P).transpose(3, 0, 2, 1).reshape(P, E * INTER),
    }
    nc = _bacc.Bacc("TRN2", target_bir_lowering=False, num_devices=1)
    launch, args = {}, []
    for name, a in arrays.items():
        a = _np.ascontiguousarray(a)
        launch[f"in_{name}"] = a
        args.append(nc.dram_tensor(f"in_{name}", a.shape, _mybir.dt.from_np(a.dtype), kind="ExternalInput").ap())
    out = nc.dram_tensor("out_x", (HALVES * SEQ, C), F32, kind="ExternalOutput").ap()
    macaron(nc, *args, out)
    r = _run(nc, [launch], core_ids=[0])
    return r.results[0]["out_x"].reshape(HALVES, SEQ, C)
```
